# Optimizing a Trainium2 kernel written in Bass

```python
import numpy as np
import jax
import jax.numpy as jnp

def _softmax(x, axis=-1):
    return jax.nn.softmax(x, axis=axis)

def _gelu(x):
    return jax.nn.gelu(x, approximate=True)

def _silu(x):
    return jax.nn.silu(x)

def _sigmoid(x):
    return jax.nn.sigmoid(x)

def _layernorm(x, axis=-1, eps=1e-05):
    m = jnp.mean(x, axis=axis, keepdims=True)
    v = jnp.var(x, axis=axis, keepdims=True)
    return (x - m) / jnp.sqrt(v + eps)

def _scatter_add(tgt, idx, src, axis=0):
    return tgt.at[idx].add(src)

def _segment_sum(src, seg, n):
    return jax.ops.segment_sum(src, seg, n)
kernel_name = 'mk_macaron_d1_jaxref_r8_368061'

def setup_inputs(seed: int=0):
    np.random.seed(seed)
    _w = jnp.asarray

    def _L0_attn_setup():
        import jax, jax.numpy as jnp
        import numpy as np
        B, T, D = (8, 512, 128)

        def log_g(x):
            return jnp.where(x >= 0, jnp.log(jnp.maximum(x, 0) + 0.5), -jax.nn.softplus(-x))
        key = jax.random.key(seed)
        kx, kf, ki, kh = jax.random.split(key, 4)
        s = 1.0 / np.sqrt(D).astype(np.float32)
        return {'x': jax.random.normal(kx, (B, T, D), dtype=jnp.float32), 'Wf': jax.random.normal(kf, (D, D), dtype=jnp.float32) * s, 'Wi': jax.random.normal(ki, (D, D), dtype=jnp.float32) * s, 'Wh': jax.random.normal(kh, (D, D), dtype=jnp.float32) * s}
    _L0_attn_in = _L0_attn_setup()

    def _L0_ffn_setup():
        import jax, jax.numpy as jnp
        import numpy as np
        EPS = 1e-08

        def _ternary_linear(x, w):
            alpha = jnp.mean(jnp.abs(w))
            w_t = jnp.sign(w) * (jnp.abs(w) > 0.5 * alpha).astype(w.dtype)
            w_q = w + jax.lax.stop_gradient(w_t - w)
            d = x.shape[-1]
            rms = jnp.sqrt(jnp.sum(x * x, axis=-1, keepdims=True)) / jnp.sqrt(jnp.asarray(d, x.dtype))
            x_norm = x / (rms + EPS)
            return jnp.einsum('bsd,fd->bsf', x_norm, w_q)
        key = jax.random.key(seed)
        k1, k2, k3 = jax.random.split(key, 3)
        d_model, d_ff = (128, 512)
        B, S = (4, 512)
        x = jax.random.normal(k1, (B, S, d_model), dtype=jnp.float32)
        w_up = jax.random.normal(k2, (d_ff, d_model), dtype=jnp.float32) * 0.02
        w_down = jax.random.normal(k3, (d_model, d_ff), dtype=jnp.float32) * 0.02
        return {'x': x, 'w_up': w_up, 'w_down': w_down}
    _L0_ffn_in = _L0_ffn_setup()
    _d = {'L0_attn_x': _L0_attn_in['x'], 'L0_attn_Wf': _L0_attn_in['Wf'], 'L0_attn_Wi': _L0_attn_in['Wi'], 'L0_attn_Wh': _L0_attn_in['Wh'], 'L0_ffn_w_up': _L0_ffn_in['w_up'], 'L0_ffn_w_down': _L0_ffn_in['w_down']}
    _x0 = _d['L0_attn_x']
    _d['L0_attn_x'] = jax.random.normal(jax.random.fold_in(jax.random.key(seed), 1), (32, 256, 128), dtype=_x0.dtype)
    del _x0
    return _d

def reference(L0_attn_x, L0_attn_Wf, L0_attn_Wi, L0_attn_Wh, L0_ffn_w_up, L0_ffn_w_down):

    def _L0_attn_ref(x, Wf, Wi, Wh):
        import jax, jax.numpy as jnp
        import numpy as np
        B, T, D = (8, 512, 128)

        def log_g(x):
            return jnp.where(x >= 0, jnp.log(jnp.maximum(x, 0) + 0.5), -jax.nn.softplus(-x))
        log_f = jax.nn.log_sigmoid(jnp.einsum('btd,ed->bte', x, Wf))
        log_i = jax.nn.log_sigmoid(jnp.einsum('btd,ed->bte', x, Wi))
        log_tilde_h = log_g(jnp.einsum('btd,ed->bte', x, Wh))
        b, t, d = x.shape
        log_h0 = jnp.full((b, 1, d), jnp.log(jnp.float32(0.5)), dtype=x.dtype)
        log_values = jnp.concatenate([log_h0, log_i + log_tilde_h], axis=1)
        a_star = jnp.concatenate([jnp.zeros((b, 1, d), x.dtype), jnp.cumsum(log_f, axis=1)], axis=1)
        log_h0_plus_b_star = jax.lax.associative_scan(jnp.logaddexp, log_values - a_star, axis=1)
        log_h = a_star + log_h0_plus_b_star
        return jnp.exp(log_h)[:, 1:]

    def _L0_ffn_ref(x, w_up, w_down):
        import jax, jax.numpy as jnp
        import numpy as np
        EPS = 1e-08

        def _ternary_linear(x, w):
            alpha = jnp.mean(jnp.abs(w))
            w_t = jnp.sign(w) * (jnp.abs(w) > 0.5 * alpha).astype(w.dtype)
            w_q = w + jax.lax.stop_gradient(w_t - w)
            d = x.shape[-1]
            rms = jnp.sqrt(jnp.sum(x * x, axis=-1, keepdims=True)) / jnp.sqrt(jnp.asarray(d, x.dtype))
            x_norm = x / (rms + EPS)
            return jnp.einsum('bsd,fd->bsf', x_norm, w_q)
        h = jax.nn.gelu(_ternary_linear(x, w_up), approximate=False)
        return _ternary_linear(h, w_down)
    x = L0_attn_x
    x = x + 0.5 * _L0_ffn_ref(_layernorm(x, axis=-1), L0_ffn_w_up, L0_ffn_w_down)
    x = x + _L0_attn_ref(_layernorm(x, axis=-1), L0_attn_Wf, L0_attn_Wi, L0_attn_Wh)
    x = x + 0.5 * _L0_ffn_ref(_layernorm(x, axis=-1), L0_ffn_w_up, L0_ffn_w_down)
    return x

_drawn_inputs = setup_inputs


def setup_inputs(seed=0):
    import zlib

    import numpy as np

    out = dict(_drawn_inputs(seed))
    spreads = {}
    factors = {}
    for name, (base, spread) in spreads.items():
        noise = np.random.default_rng([zlib.crc32(name.encode()), seed]).standard_normal(out[name].shape)
        drawn = base * np.exp(spread * noise) if base else spread * noise
        out[name] = jnp.asarray(drawn.astype(out[name].dtype))
    for name, factor in factors.items():
        out[name] = (out[name] * factor).astype(out[name].dtype)
    return out
```

```python
from contextlib import ExitStack

import concourse.bass as bass
from concourse import mybir

F32 = mybir.dt.float32
F16 = mybir.dt.float16
ALU = mybir.AluOpType
ACT = mybir.ActivationFunctionType
AXIS = mybir.AxisListType

P = 128
TILES = 4
GT = TILES * P
LN_EPS = 1e-5
RMS_EPS = 1e-8
SPLIT = 4096.0


def build_macaron(nc, x_in, w_f, w_i, w_h, w_up, w_down, x_out):
    batch, seq, d = x_in.shape
    dff = w_up.shape[0]
    chunks = dff // P
    groups = batch * seq // GT
    assert d == P and chunks == 4 and GT % seq == 0 and groups % 2 == 0
    x_src = x_in.rearrange("b s d -> (b s) d").rearrange("(n p) d -> p n d", p=P)
    x_dst = x_out.rearrange("b s d -> (b s) d").rearrange("(n p) d -> p n d", p=P)

    with ExitStack() as ctx:
        def sb(name, shape, dt=F32):
            return ctx.enter_context(nc.sbuf_tensor(name, shape, dt))

        def sem(name):
            return ctx.enter_context(nc.semaphore(name))

        X = sb("X", [P, groups * TILES, d])
        ident = sb("ident", [P, P])
        ones = sb("ones", [P, P])
        up_raw = sb("up_raw", [P, chunks, d])
        down_raw = sb("down_raw", [P, dff])
        gate_raw = sb("gate_raw", [P, 3, d])
        below = sb("below", [P, dff])
        up_t = sb("up_t", [P, dff])
        down_t = sb("down_t", [P, dff])
        abs_sum = sb("abs_sum", [P, 2])
        limit = sb("limit", [P, 4])
        up_w = sb("up_w", [P, dff], F16)
        down_w = sb("down_w", [P, chunks, d])
        gate_w = sb("gate_w", [P, 3, d])
        eps_tile = sb("eps_tile", [P, 3, TILES])
        half_tile = sb("half_tile", [P, 8])
        st = sb("st", [P, TILES, 6])
        mv_now = [sb(f"mv_now{l}", [P, 2, TILES, 2]) for l in range(3)]
        mv = [sb(f"mv{l}", [P, groups * TILES, 2]) for l in range(3)]
        rstd = [sb(f"rstd{l}", [P, groups * TILES]) for l in range(3)]
        var_eps = [sb(f"var_eps{l}", [P, 2, 8]) for l in range(3)]
        var_root = [sb(f"var_root{l}", [P, 2, 8]) for l in range(3)]
        ln_den = sb("ln_den", [P, 2, TILES])
        xn = sb("xn", [P, 2, TILES, d])
        xt_hi = sb("xt_hi", [P, 2, GT], F16)
        xt_lo = sb("xt_lo", [P, 2, GT], F16)
        h = sb("h", [P, 2, chunks, GT])
        h_sq = sb("h_sq", [P, chunks, GT])
        h_sq2 = sb("h_sq2", [P, 2, GT])
        q = sb("q", [P, 2, GT])
        ms = sb("ms", [P, 2, TILES])
        rms = sb("rms", [P, 2, TILES])
        rms_den = sb("rms_den", [P, 2, TILES])
        y_scale = sb("y_scale", [P, 2, TILES])
        xt = sb("xt", [P, 2, GT])
        sig = sb("sig", [P, 2, 3, GT])
        sig_cap = sb("sig_cap", [P, 2, GT])
        cand = sb("cand", [P, 2, GT])
        inject = sb("inject", [P, 2, GT])
        hidden = sb("hidden", [P, 2, GT])

        banks = [ctx.enter_context(nc.psum_tensor(f"bank{n}", [P, GT], F32)) for n in range(2)]
        U01 = ctx.enter_context(nc.psum_tensor("U01", [P, 2, GT], F32))
        U23 = ctx.enter_context(nc.psum_tensor("U23", [P, 2, GT], F32))
        Y = ctx.enter_context(nc.psum_tensor("Y", [P, 2, TILES, d], F32))
        T, S = banks
        U = [U01, U23]
        Z = [[U01[:, 0, :], U01[:, 1, :], U23[:, 0, :]],
             [U23[:, 1, :], Y[:, 0].rearrange("p t d -> p (t d)"), Y[:, 1].rearrange("p t d -> p (t d)")]]
        O = S

        x_loaded = [sem("x_loaded_even"), sem("x_loaded_odd")]
        x_stored = [sem("x_stored_even"), sem("x_stored_odd")]
        w_up_loaded, w_down_loaded, w_gate_loaded = sem("w_up_loaded"), sem("w_down_loaded"), sem("w_gate_loaded")
        consts_set, ident_zero = sem("consts_set"), sem("ident_zero")
        wsum_done, wtotal_done, limit_done = sem("wsum_done"), sem("wtotal_done"), sem("limit_done")
        below_done, ternary_done = sem("below_done"), sem("ternary_done")
        w_turned, w_taken = sem("w_turned"), sem("w_taken")
        mv_kept = sem("mv_kept")
        mv_done = [sem(f"mv_done{l}") for l in range(3)]
        var_set = [sem(f"var_set{l}") for l in range(3)]
        root_done = [sem(f"root_done{l}") for l in range(3)]
        rstd_done = [sem(f"rstd_done{l}") for l in range(3)]
        den_done = sem("den_done")
        xn_ready, xt_ready, xt_taken = sem("xn_ready"), sem("xt_ready"), sem("xt_taken")
        hi_ready, up_ready, gelu_done, sq_done = sem("hi_ready"), sem("up_ready"), sem("gelu_done"), sem("sq_done")
        sq2_done, q_ready = sem("sq2_done"), sem("q_ready")
        ssq_ready, ms_taken, rms_ready, y_scale_done = sem("ssq_ready"), sem("ms_taken"), sem("rms_ready"), sem("y_scale_done")
        down_done, ffn_added = sem("down_done"), sem("ffn_added")
        gate_ready, sig_done, cap_done, cand_done = sem("gate_ready"), sem("sig_done"), sem("cap_done"), sem("cand_done")
        inject_done, scan_done, turned_back, rnn_added = sem("inject_done"), sem("scan_done"), sem("turned_back"), sem("rnn_added")

        block = ctx.enter_context(nc.Block())

        def span(eng, start, stop, loop_from, loop_to, step):
            assert loop_from % 2 == 0 and loop_to % 2 == 0
            for k in range(start, loop_from):
                step(k, k % 2, lambda g: 0 <= g < groups)
            with eng.Fori(loop_from // 2, loop_to // 2) as pair:
                for j in range(2):
                    step(pair * 2 + j, j, lambda g: True)
            for k in range(loop_to, stop):
                step(k, k % 2, lambda g: 0 <= g < groups)

        def wait_alone(eng, semaphore, value):
            if not isinstance(value, int):
                value = eng.snap(value)
                eng.wait_ge(consts_set, 3)
            eng.wait_ge(semaphore, value)

        def tile_cols(g, n=TILES, t=0):
            return bass.ds(g * TILES + t, n)

        @block.sync
        def _(sp):
            def load(g, par):
                sp.dma_start(X[:, tile_cols(g), :], x_src[:, tile_cols(g), :]).then_inc(x_loaded[par], 16)

            load(0, 0)
            load(1, 1)
            with sp.Fori(1, groups // 2) as pair:
                for j in range(2):
                    sp.wait_ge(x_loaded[j], pair * 16)
                    load(pair * 2 + j, j)
            with sp.Fori(0, groups // 2) as pair:
                for j in range(2):
                    sp.wait_ge(ffn_added, pair * 2 + (groups + 1 + j))
                    g = pair * 2 + j
                    sp.dma_start(x_dst[:, tile_cols(g), :], X[:, tile_cols(g), :]).then_inc(x_stored[j], 16)
            for j in range(2):
                sp.wait_ge(x_stored[j], 16 * (groups // 2))

        @block.gpsimd
        def _(pool):
            nc.gpsimd.memset(ident[:], 0.0).then_inc(ident_zero, 1)
            nc.gpsimd.memset(ones[:], 1.0).then_inc(consts_set, 1)
            nc.gpsimd.memset(half_tile[:], 0.5).then_inc(consts_set, 1)
            for n, value in enumerate((LN_EPS, LN_EPS * SPLIT ** -2, SPLIT ** -2)):
                nc.gpsimd.memset(eps_tile[:, n, :], value).then_inc(consts_set, 1)
            pool.wait_ge(ident_zero, 1)
            nc.gpsimd.affine_select(out=ident[:], in_=ident[:], compare_op=ALU.not_equal, fill=1.0, base=0,
                                    pattern=[[-1, P]], channel_multiplier=1).then_inc(consts_set, 1)
            pool.wait_ge(consts_set, 6)

            def ln_roots(l, g, par):
                pool.wait_ge(mv_done[l], g + 1)
                var = mv_now[l][:, par, :, 1]
                if l == 1:
                    nc.gpsimd.tensor_tensor(var_eps[l][:, par, 0:4], var, eps_tile[:, 0, :], ALU.add).then_inc(var_set[l], 1)
                else:
                    nc.gpsimd.tensor_tensor(var_eps[l][:, par, 4:8], var, eps_tile[:, 2, :], ALU.mult).then_inc(var_set[l], 1)
                    pool.wait_ge(var_set[l], g * 2 + 1)
                    nc.gpsimd.tensor_tensor(var_eps[l][:, par, 0:4], var_eps[l][:, par, 4:8], eps_tile[:, 1, :],
                                            ALU.add).then_inc(var_set[l], 1)
                per = 1 if l == 1 else 2
                pool.wait_ge(var_set[l], g * per + per)
                nc.gpsimd.tensor_tensor(var_root[l][:, par, 0:4 * per], var_eps[l][:, par, 0:4 * per],
                                        half_tile[:, 0:4 * per], ALU.pow).then_inc(root_done[l], 1)

            def rms_root(F, par):
                pool.wait_ge(ms_taken, F + 1)
                nc.gpsimd.tensor_tensor(rms[:, par, :], ms[:, par, :], half_tile[:, 0:TILES],
                                        ALU.pow).then_inc(rms_ready, 1)

            def ffn1(k, par, on):
                if on(k - 2):
                    ln_roots(1, k - 2, par)
                if on(k + 3):
                    ln_roots(0, k + 3, 1 - par)
                if on(k - 1):
                    rms_root(k - 1, 1 - par)

            def rnn(k, par, on):
                if on(k):
                    pool.wait_ge(sig_done, k * 3 + 1)
                if on(k - 1):
                    pool.wait_ge(cand_done, k)
                    pool.wait_ge(sig_done, k * 3 - 1)
                    nc.gpsimd.tensor_tensor(inject[:, 1 - par, :], sig[:, 1 - par, 1, :], cand[:, 1 - par, :],
                                            ALU.mult).then_inc(inject_done, 1)
                if on(k):
                    nc.gpsimd.tensor_scalar(sig_cap[:, par, :], sig[:, par, 0, :], 0.5, 0.0,
                                            ALU.min, ALU.max).then_inc(cap_done, 1)
                if on(k - 2):
                    ln_roots(2, k - 2, par)

            def ffn2(k, par, on):
                if on(k - 1):
                    rms_root(k - 1 + groups, 1 - par)

            span(pool, -3, groups + 2, 2, groups - 4, ffn1)
            span(pool, 0, groups + 2, 2, groups, rnn)
            span(pool, 1, groups + 1, 2, groups, ffn2)

        @block.scalar
        def _(act):
            nc.scalar.dma_start(up_raw[:], w_up.rearrange("(c p) d -> p c d", p=P)).then_inc(w_up_loaded, 16)
            nc.scalar.dma_start(down_raw[:], w_down).then_inc(w_down_loaded, 16)
            for n, w in enumerate((w_h, w_i, w_f)):
                nc.scalar.dma_start(gate_raw[:, n, :], w).then_inc(w_gate_loaded, 16)
            act.preload_act_table(ACT.Gelu)
            act.wait_ge(w_turned, 1)
            nc.scalar.copy(up_w[:], U01[:, 0, :]).then_inc(w_taken, 1)
            act.wait_ge(w_turned, 2)
            nc.scalar.copy(down_w[:].rearrange("p c d -> p (c d)"), U01[:, 1, :]).then_inc(w_taken, 1)
            act.wait_ge(w_turned, 3)
            nc.scalar.copy(gate_w[:].rearrange("p g d -> p (g d)"), U23[:, 0, 0:3 * d]).then_inc(w_taken, 1)

            def ffn(second):
                off = groups if second else 0
                base = 2 * groups if second else 0

                def hi(g, par):
                    act.wait_ge(xt_ready, g + base + 1)
                    if second or not isinstance(g, int) or g >= 2:
                        act.wait_ge(up_ready, (g + off) * 2 - 2)
                    nc.scalar.copy(xt_hi[:, par, :], T[:]).then_inc(hi_ready, 1)

                def step(k, par, on):
                    if on(k):
                        F = k + off
                        for half in range(2):
                            act.wait_ge(up_ready, F * 2 + half + 1)
                            if half == 0 and (second or not isinstance(k, int) or k >= 2):
                                act.wait_ge(down_done, F - 1)
                            nc.scalar.activation(h[:, par, 2 * half:2 * half + 2, :], U[half][:], ACT.Gelu,
                                                 scale=1.0 / SPLIT).then_inc(gelu_done, 1)
                    if on(k + 1):
                        hi(k + 1, 1 - par)
                    if on(k):
                        if second or not isinstance(k, int) or k >= 1:
                            act.wait_ge(sq2_done, F)
                        for half in range(2):
                            act.wait_ge(gelu_done, F * 2 + half + 1)
                            nc.scalar.activation(h_sq[:, 2 * half:2 * half + 2, :],
                                                 h[:, par, 2 * half:2 * half + 2, :],
                                                 ACT.Square).then_inc(sq_done, 1)
                span(act, -1, groups, 2, groups - 2, step)

            def rnn(k, par, on):
                if on(k + 1):
                    act.wait_ge(xt_ready, k + 1 + groups + 1)
                    if not isinstance(k, int) or k + 1 >= 2:
                        act.wait_ge(gate_ready, k * 3)
                    nc.scalar.copy(xt[:, 1 - par, :], T[:]).then_inc(xt_taken, 1)
                if on(k):
                    for n in range(3):
                        act.wait_ge(gate_ready, k * 3 + n + 1)
                        if n == 0 and (not isinstance(k, int) or k >= 2):
                            act.wait_ge(scan_done, k * 2 - 2)
                        nc.scalar.activation(sig[:, par, n, :], Z[par][n], ACT.Sigmoid).then_inc(sig_done, 1)

            ffn(False)
            act.preload_act_table(ACT.Sigmoid)
            span(act, -1, groups, 2, groups - 2, rnn)
            act.preload_act_table(ACT.Gelu)
            ffn(True)

        @block.tensor
        def _(pe):
            pe.wait_ge(consts_set, 6)
            pe.wait_ge(wsum_done, 2)
            pe.matmul(S[:, 0:2], ones[:], abs_sum[:], start=True, stop=True).then_inc(wtotal_done, 1)
            pe.wait_ge(ternary_done, 1)
            for c in range(chunks):
                t = pe.transpose(U01[:, 0, c * P:(c + 1) * P], up_t[:, c * P:(c + 1) * P], ident[:])
            t.then_inc(w_turned, 1)
            pe.wait_ge(ternary_done, 2)
            for c in range(chunks):
                t = pe.transpose(U01[:, 1, c * P:(c + 1) * P], down_t[:, c * P:(c + 1) * P], ident[:])
            t.then_inc(w_turned, 1)
            pe.wait_ge(w_gate_loaded, 48)
            for n in range(3):
                t = pe.transpose(U23[:, 0, n * P:(n + 1) * P], gate_raw[:, n, :], ident[:])
            t.then_inc(w_turned, 1)
            pe.wait_ge(w_taken, 3)

            def turn(g, par, base):
                pe.wait_ge(xn_ready, g + base + 1)
                if base or not isinstance(g, int) or g >= 1:
                    pe.wait_ge(xt_taken, g + base)
                for t in range(TILES):
                    m = pe.transpose(T[:, t * P:(t + 1) * P], xn[:, par, t, :], ident[:])
                m.then_inc(xt_ready, 1)

            def ffn(second):
                off = groups if second else 0
                base = 2 * groups if second else 0

                def up(g, par):
                    F = g + off
                    pe.wait_ge(xt_taken, g + base + 1)
                    for half in range(2):
                        if second or not isinstance(g, int) or g >= 1:
                            pe.wait_ge(gelu_done, F * 2 + half - 1)
                        for c in range(2):
                            f0 = (2 * half + c) * P
                            pe.matmul(U[half][:, c, :], up_w[:, f0:f0 + P], xt_hi[:, par, :], start=True, stop=False)
                            m = pe.matmul(U[half][:, c, :], up_w[:, f0:f0 + P], xt_lo[:, par, :], start=False, stop=True)
                        m.then_inc(up_ready, 1)

                def down(g, par):
                    F = g + off
                    pe.wait_ge(q_ready, F + 1)
                    if second or not isinstance(g, int) or g >= 1:
                        pe.wait_ge(ms_taken, F)
                    for t in range(TILES):
                        m = pe.matmul(S[:, t:t + 1], q[:, par, t * P:(t + 1) * P], ones[:, 0:1], start=True, stop=True)
                    m.then_inc(ssq_ready, 1)
                    if second or not isinstance(g, int) or g >= 2:
                        pe.wait_ge(ffn_added, F - 1)
                    for t in range(TILES):
                        for c in range(chunks):
                            m = pe.matmul(Y[:, par, t, :], h[:, par, c, t * P:(t + 1) * P], down_w[:, c, :],
                                          start=(c == 0), stop=(c == chunks - 1))
                    m.then_inc(down_done, 1)

                def step(k, par, on):
                    if on(k):
                        up(k, par)
                    if on(k + 1):
                        turn(k + 1, 1 - par, base)
                    if on(k - 1):
                        down(k - 1, 1 - par)

                if second:
                    pe.wait_ge(sig_done, 3 * groups)
                    pe.wait_ge(cand_done, groups)
                    pe.wait_ge(rnn_added, groups)
                span(pe, -1, groups + 1, 2, groups - 2, step)

            def rnn(k, par, on):
                if on(k):
                    pe.wait_ge(xt_taken, k + groups + 1)
                    if isinstance(k, int) and k == 0:
                        pe.wait_ge(gelu_done, 2 * groups)
                    if isinstance(k, int) and k == 1:
                        pe.wait_ge(ffn_added, groups)
                    if not isinstance(k, int) or k >= 2:
                        pe.wait_ge(sig_done, k * 3 - 3)
                        pe.wait_ge(cand_done, k - 1)
                    for n in range(3):
                        pe.matmul(Z[par][n], gate_w[:, n, :], xt[:, par, :], start=True, stop=True).then_inc(gate_ready, 1)
                if on(k + 1):
                    turn(k + 1, 1 - par, groups)
                if on(k - 1):
                    pe.wait_ge(scan_done, k * 2)
                    if isinstance(k, int) and k == 1:
                        pe.wait_ge(ms_taken, groups)
                    else:
                        pe.wait_ge(rnn_added, k - 1)
                    for t in range(TILES):
                        m = pe.transpose(O[:, t * P:(t + 1) * P], hidden[:, 1 - par, t * P:(t + 1) * P], ident[:])
                    m.then_inc(turned_back, 1)

            ffn(False)
            span(pe, -1, groups + 1, 2, groups - 2, rnn)
            ffn(True)

        @block.vector
        def _(dve):
            vec = nc.vector

            def ternary(n, raw, out, loaded):
                vec.tensor_scalar(below[:], raw, limit[:, 2 * n + 1:2 * n + 2], None, ALU.is_lt).then_inc(below_done, 1)
                dve.wait_ge(below_done, n + 1)
                vec.scalar_tensor_tensor(out=out[:], in0=raw, scalar=limit[:, 2 * n:2 * n + 1], in1=below[:],
                                         op0=ALU.is_gt, op1=ALU.subtract).then_inc(ternary_done, 1)

            def prepare_weights():
                up_flat = up_raw[:].rearrange("p c d -> p (c d)")
                dve.wait_ge(w_up_loaded, 16)
                vec.tensor_reduce(abs_sum[:, 0:1], up_flat, AXIS.X, ALU.add, apply_absolute_value=True).then_inc(wsum_done, 1)
                dve.wait_ge(w_down_loaded, 16)
                vec.tensor_reduce(abs_sum[:, 1:2], down_raw[:], AXIS.X, ALU.add, apply_absolute_value=True).then_inc(wsum_done, 1)
                dve.wait_ge(wtotal_done, 1)
                for n in range(2):
                    for sign in range(2):
                        vec.tensor_scalar(limit[:, 2 * n + sign:2 * n + sign + 1], S[:, n:n + 1],
                                          (0.5 if sign == 0 else -0.5) / (dff * d), None, ALU.mult).then_inc(limit_done, 1)
                dve.wait_ge(limit_done, 4)
                ternary(0, up_flat, up_t, w_up_loaded)
                dve.wait_ge(ternary_done, 1)
                ternary(1, down_raw[:], down_t, w_down_loaded)

            stats_made = [0]

            def stats(l, g, par, x_written, count):
                wait_alone(dve, x_written, count)
                for t in range(TILES):
                    m = vec.bn_stats(st[:, t, :], X[:, tile_cols(g, 1, t), :])
                dve.drain()
                for t in range(TILES):
                    m = vec.bn_aggr(mv_now[l][:, par, t, :], st[:, t, :])
                m.then_inc(mv_done[l], 1)
                dve.wait_ge(mv_done[l], g + 1)
                vec.tensor_copy(mv[l][:, tile_cols(g), :], mv_now[l][:, par, :, :]).then_inc(mv_kept, 1)

            def ln_scale(l, g, par, den_before):
                dve.wait_ge(root_done[l], g + 1)
                if l == 1:
                    src = var_root[l][:, par, 0:4]
                else:
                    vec.scalar_tensor_tensor(out=ln_den[:, par, :], in0=var_root[l][:, par, 0:4], scalar=RMS_EPS,
                                             in1=var_root[l][:, par, 4:8], op0=ALU.mult, op1=ALU.add).then_inc(den_done, 1)
                    dve.wait_ge(den_done, den_before + 1)
                    src = ln_den[:, par, :]
                vec.reciprocal(rstd[l][:, tile_cols(g)], src).then_inc(rstd_done[l], 1)

            def norm(l, g, par):
                dve.wait_ge(rstd_done[l], g + 1)
                if l or not isinstance(g, int) or g >= 2:
                    dve.wait_ge(xt_ready, g + l * groups - 1)
                for t in range(TILES):
                    m = vec.tensor_scalar(xn[:, par, t, :], X[:, tile_cols(g, 1, t), :].rearrange("p a d -> p (a d)"),
                                          mv[l][:, tile_cols(g, 1, t), 0], rstd[l][:, tile_cols(g, 1, t)],
                                          ALU.subtract, ALU.mult)
                m.then_inc(xn_ready, 1)

            def low_part(g, par, l):
                dve.wait_ge(hi_ready, g + (groups if l else 0) + 1)
                vec.tensor_tensor(xt_lo[:, par, :], T[:], xt_hi[:, par, :], ALU.subtract).then_inc(xt_taken, 1)

            def sum_squares(F, par):
                dve.wait_ge(sq_done, F * 2 + 2)
                vec.tensor_tensor(h_sq2[:], h_sq[:, 0:2, :], h_sq[:, 2:4, :], ALU.add).then_inc(sq2_done, 1)

            def sum_squares2(F, par):
                dve.wait_ge(sq2_done, F + 1)
                if not isinstance(F, int) or F >= 2:
                    dve.wait_ge(ssq_ready, F - 1)
                vec.tensor_tensor(q[:, par, :], h_sq2[:, 0, :], h_sq2[:, 1, :], ALU.add).then_inc(q_ready, 1)

            def mean_square(F, par):
                dve.wait_ge(ssq_ready, F + 1)
                vec.tensor_scalar(ms[:, par, :], S[:, 0:TILES], 1.0 / dff, None, ALU.mult).then_inc(ms_taken, 1)

            def add_ffn(F, g, par, den_before):
                dve.wait_ge(rms_ready, F + 1)
                vec.tensor_scalar(rms_den[:, par, :], rms[:, par, :], RMS_EPS, 2.0, ALU.add, ALU.mult).then_inc(den_done, 1)
                dve.wait_ge(den_done, den_before + 1)
                vec.reciprocal(y_scale[:, par, :], rms_den[:, par, :]).then_inc(y_scale_done, 1)
                dve.wait_ge(y_scale_done, F + 1)
                dve.wait_ge(down_done, F + 1)
                for t in range(TILES):
                    xt_ = X[:, tile_cols(g, 1, t), :].rearrange("p a d -> p (a d)")
                    m = vec.scalar_tensor_tensor(out=xt_, in0=Y[:, par, t, :], scalar=y_scale[:, par, t:t + 1], in1=xt_,
                                                 op0=ALU.mult, op1=ALU.add)
                m.then_inc(ffn_added, 1)

            def made(k, lags):
                if isinstance(k, int):
                    return sum(min(max(k + lag, 0), groups) for lag in lags)
                return k * len(lags) + sum(lags)

            def ffn1(k, par, on):
                if on(k - 2):
                    add_ffn(k - 2, k - 2, par, made(k, [-2, 2]))
                    stats(1, k - 2, par, ffn_added, k - 1)
                if on(k - 3):
                    ln_scale(1, k - 3, 1 - par, 0)
                if on(k + 2):
                    ln_scale(0, k + 2, par, made(k, [2]) + made(k + 1, [-2]))
                    norm(0, k + 2, par)
                if on(k + 3):
                    stats(0, k + 3, 1 - par, x_loaded[1 - par], (k + 3) * 8 + (16 if par else 8))
                if on(k + 1):
                    low_part(k + 1, 1 - par, 0)
                if on(k - 1):
                    mean_square(k - 1, 1 - par)
                if on(k):
                    sum_squares(k, par)
                    sum_squares2(k, par)

            den1 = 2 * groups

            def rnn(k, par, on):
                if on(k - 2):
                    dve.wait_ge(turned_back, k - 1)
                    cols = tile_cols(k - 2)
                    vec.tensor_tensor(X[:, cols, :], O[:].rearrange("p (t d) -> p t d", d=d), X[:, cols, :],
                                      ALU.add).then_inc(rnn_added, 1)
                    stats(2, k - 2, par, rnn_added, k - 1)
                if on(k - 3):
                    ln_scale(2, k - 3, 1 - par, den1 + made(k, [-3]))
                if on(k + 2):
                    norm(1, k + 2, par)
                if on(k):
                    dve.wait_ge(cap_done, k + 1)
                    if not isinstance(k, int) or k >= 2:
                        dve.wait_ge(inject_done, k - 1)
                    vec.scalar_tensor_tensor(out=cand[:, par, :], in0=Z[par][0], scalar=0.0, in1=sig_cap[:, par, :],
                                             op0=ALU.max, op1=ALU.add).then_inc(cand_done, 1)
                if on(k - 1):
                    dve.wait_ge(inject_done, k)
                    dve.wait_ge(sig_done, k * 3)
                    if not isinstance(k, int) or k >= 3:
                        dve.wait_ge(turned_back, k - 2)
                    for b in range(GT // seq):
                        cols = slice(b * seq, (b + 1) * seq)
                        vec.tensor_tensor_scan(hidden[:, 1 - par, cols], sig[:, 1 - par, 2, cols],
                                               inject[:, 1 - par, cols], 0.5, ALU.mult, ALU.add).then_inc(scan_done, 1)

            def ffn2(k, par, on):
                if on(k - 2):
                    add_ffn(k - 2 + groups, k - 2, par, den1 + groups + made(k, [-2]))
                if on(k + 2):
                    norm(2, k + 2, par)
                if on(k + 1):
                    low_part(k + 1, 1 - par, 2)
                if on(k - 1):
                    mean_square(k - 1 + groups, 1 - par)
                if on(k):
                    sum_squares(k + groups, par)
                    sum_squares2(k + groups, par)

            prepare_weights()
            span(dve, -3, groups + 3, 4, groups - 4, ffn1)
            span(dve, -2, groups + 3, 4, groups - 2, rnn)
            span(dve, -2, groups + 2, 2, groups - 2, ffn2)


def kernel(**inputs):
    import numpy as np
    import concourse.bacc as bacc
    from concourse.bass_utils import run_bass_kernel_spmd as run

    names = ["L0_attn_x", "L0_attn_Wf", "L0_attn_Wi", "L0_attn_Wh", "L0_ffn_w_up", "L0_ffn_w_down"]
    nc = bacc.Bacc("TRN2", target_bir_lowering=False, num_devices=1)
    arrays, args = {}, []
    for name in names:
        a = np.ascontiguousarray(inputs[name])
        arrays[f"in_{name}"] = a
        args.append(nc.dram_tensor(f"in_{name}", a.shape, mybir.dt.from_np(a.dtype), kind="ExternalInput").ap())
    out = nc.dram_tensor("out_x", arrays["in_L0_attn_x"].shape, F32, kind="ExternalOutput").ap()
    build_macaron(nc, *args, out)
    return run(nc, [arrays], core_ids=[0]).results[0]["out_x"]
```

```python
from contextlib import ExitStack

import concourse.bass as bass
from concourse import mybir

F32 = mybir.dt.float32
F16 = mybir.dt.float16
ALU = mybir.AluOpType
ACT = mybir.ActivationFunctionType
AXIS = mybir.AxisListType

P = 128
TILES = 4
GT = TILES * P
LN_EPS = 1e-5
RMS_EPS = 1e-8
SPLIT = 4096.0


def build_macaron(nc, x_in, w_f, w_i, w_h, w_up, w_down, x_out):
    batch, seq, d = x_in.shape
    dff = w_up.shape[0]
    chunks = dff // P
    groups = batch * seq // GT
    assert d == P and chunks == 4 and GT % seq == 0 and groups % 2 == 0
    x_src = x_in.rearrange("b s d -> (b s) d").rearrange("(n p) d -> p n d", p=P)
    x_dst = x_out.rearrange("b s d -> (b s) d").rearrange("(n p) d -> p n d", p=P)

    with ExitStack() as ctx:
        def sb(name, shape, dt=F32):
            return ctx.enter_context(nc.sbuf_tensor(name, shape, dt))

        def sem(name):
            return ctx.enter_context(nc.semaphore(name))

        X = sb("X", [P, groups * TILES, d])
        ident = sb("ident", [P, P])
        ones = sb("ones", [P, P])
        up_raw = sb("up_raw", [P, chunks, d])
        down_raw = sb("down_raw", [P, dff])
        gate_raw = sb("gate_raw", [P, 3, d])
        below = sb("below", [P, dff])
        up_t = sb("up_t", [P, dff])
        down_t = sb("down_t", [P, dff])
        abs_sum = sb("abs_sum", [P, 2])
        limit = sb("limit", [P, 4])
        up_w = sb("up_w", [P, dff], F16)
        down_w = sb("down_w", [P, chunks, d])
        gate_w = sb("gate_w", [P, 3, d])
        eps_tile = sb("eps_tile", [P, 3, TILES])
        half_tile = sb("half_tile", [P, 8])
        st = [sb(f"st{l}", [P, 2, TILES, 6]) for l in range(3)]
        mv_now = [sb(f"mv_now{l}", [P, 2, TILES, 2]) for l in range(3)]
        rstd = [sb(f"rstd{l}", [P, groups * TILES]) for l in range(3)]
        shift = [sb(f"shift{l}", [P, groups * TILES]) for l in range(3)]
        var_eps = [sb(f"var_eps{l}", [P, 2, 8]) for l in range(3)]
        var_root = [sb(f"var_root{l}", [P, 2, 8]) for l in range(3)]
        ln_den = sb("ln_den", [P, 2, TILES])
        xn = sb("xn", [P, 2, TILES, d])
        xt_hi = sb("xt_hi", [P, 2, GT], F16)
        xt_lo = sb("xt_lo", [P, 2, GT], F16)
        h = sb("h", [P, 2, chunks, GT])
        h_sq = sb("h_sq", [P, chunks, GT])
        h_sq2 = sb("h_sq2", [P, 2, GT])
        q = sb("q", [P, 2, GT])
        ms = sb("ms", [P, 2, TILES])
        rms = sb("rms", [P, 2, TILES])
        rms_den = sb("rms_den", [P, 2, TILES])
        y_scale = sb("y_scale", [P, 2, TILES])
        xt = sb("xt", [P, 2, GT])
        sig = sb("sig", [P, 2, 3, GT])
        relu_z = sb("relu_z", [P, 2, GT])
        cand = sb("cand", [P, 2, GT])
        inject = sb("inject", [P, 2, GT])
        hidden = sb("hidden", [P, 2, GT])

        banks = [ctx.enter_context(nc.psum_tensor(f"bank{n}", [P, GT], F32)) for n in range(2)]
        U01 = ctx.enter_context(nc.psum_tensor("U01", [P, 2, GT], F32))
        U23 = ctx.enter_context(nc.psum_tensor("U23", [P, 2, GT], F32))
        Y = ctx.enter_context(nc.psum_tensor("Y", [P, 2, TILES, d], F32))
        T, S = banks
        U = [U01, U23]
        Z = [[U01[:, 0, :], U01[:, 1, :], U23[:, 0, :]],
             [U23[:, 1, :], Y[:, 0].rearrange("p t d -> p (t d)"), Y[:, 1].rearrange("p t d -> p (t d)")]]
        O = S

        x_loaded = [sem("x_loaded_even"), sem("x_loaded_odd")]
        x_stored = [sem("x_stored_even"), sem("x_stored_odd")]
        w_up_loaded, w_down_loaded, w_gate_loaded = sem("w_up_loaded"), sem("w_down_loaded"), sem("w_gate_loaded")
        consts_set, ident_zero = sem("consts_set"), sem("ident_zero")
        wsum_done, wtotal_done, limit_done = sem("wsum_done"), sem("wtotal_done"), sem("limit_done")
        below_done, ternary_done = sem("below_done"), sem("ternary_done")
        w_turned, w_taken = sem("w_turned"), sem("w_taken")
        mv_done = [sem(f"mv_done{l}") for l in range(3)]
        var_set = [sem(f"var_set{l}") for l in range(3)]
        root_done = [sem(f"root_done{l}") for l in range(3)]
        rstd_done = [sem(f"rstd_done{l}") for l in range(3)]
        shift_done = [sem(f"shift_done{l}") for l in range(3)]
        den_done, rms_den_done = sem("den_done"), sem("rms_den_done")
        xn_ready, xt_ready, xt_taken = sem("xn_ready"), sem("xt_ready"), sem("xt_taken")
        hi_ready, up_ready, gelu_done, sq_done = sem("hi_ready"), sem("up_ready"), sem("gelu_done"), sem("sq_done")
        sq2_done, q_ready = sem("sq2_done"), sem("q_ready")
        ssq_ready, ms_taken, rms_ready, y_scale_done = sem("ssq_ready"), sem("ms_taken"), sem("rms_ready"), sem("y_scale_done")
        down_done, ffn_added = sem("down_done"), sem("ffn_added")
        gate_ready, sig_done, cand_done = sem("gate_ready"), sem("sig_done"), sem("cand_done")
        inject_done, scan_done, turned_back, rnn_added = sem("inject_done"), sem("scan_done"), sem("turned_back"), sem("rnn_added")

        block = ctx.enter_context(nc.Block())

        def span(eng, start, stop, loop_from, loop_to, step):
            assert loop_from % 2 == 0 and loop_to % 2 == 0
            for k in range(start, loop_from):
                step(k, k % 2, lambda g: 0 <= g < groups)
            with eng.Fori(loop_from // 2, loop_to // 2) as pair:
                for j in range(2):
                    step(pair * 2 + j, j, lambda g: True)
            for k in range(loop_to, stop):
                step(k, k % 2, lambda g: 0 <= g < groups)

        def wait_alone(eng, *waits):
            if not all(isinstance(value, int) for _, value in waits):
                waits = [(semaphore, eng.snap(value)) for semaphore, value in waits]
                eng.wait_ge(consts_set, 3)
            for semaphore, value in waits:
                eng.wait_ge(semaphore, value)

        def tile_cols(g, n=TILES, t=0):
            return bass.ds(g * TILES + t, n)

        @block.sync
        def _(sp):
            def load(g, par):
                sp.dma_start(X[:, tile_cols(g), :], x_src[:, tile_cols(g), :]).then_inc(x_loaded[par], 16)

            load(0, 0)
            load(1, 1)
            with sp.Fori(1, groups // 2) as pair:
                for j in range(2):
                    sp.wait_ge(x_loaded[j], pair * 16)
                    load(pair * 2 + j, j)
            with sp.Fori(0, groups // 2) as pair:
                for j in range(2):
                    sp.wait_ge(ffn_added, pair * 2 + (groups + 1 + j))
                    g = pair * 2 + j
                    sp.dma_start(x_dst[:, tile_cols(g), :], X[:, tile_cols(g), :]).then_inc(x_stored[j], 16)
            for j in range(2):
                sp.wait_ge(x_stored[j], 16 * (groups // 2))

        @block.gpsimd
        def _(pool):
            nc.gpsimd.memset(ident[:], 0.0).then_inc(ident_zero, 1)
            nc.gpsimd.memset(ones[:], 1.0).then_inc(consts_set, 1)
            nc.gpsimd.memset(half_tile[:], 0.5).then_inc(consts_set, 1)
            for n, value in enumerate((LN_EPS, LN_EPS * SPLIT ** -2, SPLIT ** -2)):
                nc.gpsimd.memset(eps_tile[:, n, :], value).then_inc(consts_set, 1)
            pool.wait_ge(ident_zero, 1)
            nc.gpsimd.affine_select(out=ident[:], in_=ident[:], compare_op=ALU.not_equal, fill=1.0, base=0,
                                    pattern=[[-1, P]], channel_multiplier=1).then_inc(consts_set, 1)
            pool.wait_ge(consts_set, 6)

            def ln_roots(l, g, par):
                pool.wait_ge(mv_done[l], g + 1)
                var = mv_now[l][:, par, :, 1]
                if l == 1:
                    nc.gpsimd.tensor_tensor(var_eps[l][:, par, 0:4], var, eps_tile[:, 0, :], ALU.add).then_inc(var_set[l], 1)
                else:
                    nc.gpsimd.tensor_tensor(var_eps[l][:, par, 4:8], var, eps_tile[:, 2, :], ALU.mult).then_inc(var_set[l], 1)
                    pool.wait_ge(var_set[l], g * 2 + 1)
                    nc.gpsimd.tensor_tensor(var_eps[l][:, par, 0:4], var_eps[l][:, par, 4:8], eps_tile[:, 1, :],
                                            ALU.add).then_inc(var_set[l], 1)
                per = 1 if l == 1 else 2
                pool.wait_ge(var_set[l], g * per + per)
                nc.gpsimd.tensor_tensor(var_root[l][:, par, 0:4 * per], var_eps[l][:, par, 0:4 * per],
                                        half_tile[:, 0:4 * per], ALU.pow).then_inc(root_done[l], 1)

            def rms_root(F, par):
                pool.wait_ge(ms_taken, F + 1)
                nc.gpsimd.tensor_tensor(rms[:, par, :], ms[:, par, :], half_tile[:, 0:TILES],
                                        ALU.pow).then_inc(rms_ready, 1)

            def add_squares(F, par):
                pool.wait_ge(sq2_done, F * 2 + 2)
                if not isinstance(F, int) or F >= 2:
                    pool.wait_ge(ssq_ready, F - 1)
                nc.gpsimd.tensor_tensor(q[:, par, :], h_sq2[:, 0, :], h_sq2[:, 1, :], ALU.add).then_inc(q_ready, 1)

            def ffn1(k, par, on):
                if on(k - 2):
                    ln_roots(1, k - 2, par)
                if on(k - 1):
                    rms_root(k - 1, 1 - par)
                if on(k):
                    add_squares(k, par)
                if on(k + 4):
                    ln_roots(0, k + 4, par)

            def rnn(k, par, on):
                if on(k):
                    pool.wait_ge(cand_done, k + 1)
                    pool.wait_ge(sig_done, k * 4 + 3)
                    nc.gpsimd.tensor_tensor(inject[:, par, :], sig[:, par, 1, :], cand[:, par, :],
                                            ALU.mult).then_inc(inject_done, 1)
                if on(k - 3):
                    ln_roots(2, k - 3, 1 - par)

            def ffn2(k, par, on):
                if on(k - 1):
                    rms_root(k - 1 + groups, 1 - par)
                if on(k):
                    add_squares(k + groups, par)

            span(pool, -4, groups + 2, 2, groups - 4, ffn1)
            span(pool, 0, groups + 3, 4, groups, rnn)
            span(pool, 0, groups + 1, 2, groups, ffn2)

        @block.scalar
        def _(act):
            nc.scalar.dma_start(up_raw[:], w_up.rearrange("(c p) d -> p c d", p=P)).then_inc(w_up_loaded, 16)
            nc.scalar.dma_start(down_raw[:], w_down).then_inc(w_down_loaded, 16)
            for n, w in enumerate((w_h, w_i, w_f)):
                nc.scalar.dma_start(gate_raw[:, n, :], w).then_inc(w_gate_loaded, 16)
            act.preload_act_table(ACT.Gelu)
            def take_weights(n):
                act.wait_ge(w_turned, n + 1)
                out, src = ((up_w[:], Y[:, 0]), (down_w[:], Y[:, 1]),
                            (gate_w[:], S[:, 0:3 * d].rearrange("p (g d) -> p g d", d=d)))[n]
                nc.scalar.copy(out, src if n else src.rearrange("p t d -> p (t d)")).then_inc(w_taken, 1)

            def norm(l, g, par):
                older = [(xt_ready, g + l * groups - 1)] if l or not isinstance(g, int) or g >= 2 else []
                wait_alone(act, (shift_done[l], g + 1), *older)
                for t in range(TILES):
                    m = nc.scalar.activation(xn[:, par, t, :], X[:, tile_cols(g, 1, t), :].rearrange("p a d -> p (a d)"),
                                             ACT.Identity, bias=shift[l][:, tile_cols(g, 1, t)],
                                             scale=rstd[l][:, tile_cols(g, 1, t)])
                m.then_inc(xn_ready, 1)

            def ffn(second):
                off = groups if second else 0
                base = 2 * groups if second else 0

                def hi(g, par):
                    act.wait_ge(xt_ready, g + base + 1)
                    if second or not isinstance(g, int) or g >= 2:
                        act.wait_ge(up_ready, (g + off) * 2 - 2)
                    nc.scalar.copy(xt_hi[:, par, :], T[:]).then_inc(hi_ready, 1)

                def gelu(g, par, half):
                    F = g + off
                    act.wait_ge(up_ready, F * 2 + half + 1)
                    if half == 0 and (second or not isinstance(g, int) or g >= 2):
                        act.wait_ge(down_done, F - 1)
                    nc.scalar.activation(h[:, par, 2 * half:2 * half + 2, :], U[half][:], ACT.Gelu,
                                         scale=1.0 / SPLIT).then_inc(gelu_done, 1)

                def square(g, par, half):
                    F = g + off
                    act.wait_ge(gelu_done, F * 2 + half + 1)
                    if second or not isinstance(g, int) or g >= 1:
                        act.wait_ge(sq2_done, F * 2 + half - 1)
                    nc.scalar.activation(h_sq[:, 2 * half:2 * half + 2, :], h[:, par, 2 * half:2 * half + 2, :],
                                         ACT.Square).then_inc(sq_done, 1)

                def step(k, par, on):
                    if not second and isinstance(k, int) and k == -2:
                        take_weights(0)
                    if on(k):
                        gelu(k, par, 0)
                        square(k, par, 0)
                        gelu(k, par, 1)
                    if on(k + 1) and not (second and isinstance(k, int) and k == 0):
                        hi(k + 1, 1 - par)
                    if second and isinstance(k, int) and k == -1:
                        hi(1, 1)
                    if on(k):
                        square(k, par, 1)
                    if on(k + 2) and not second:
                        norm(0, k + 2, par)
                    elif on(k) and not second:
                        norm(1, k + 2 - groups, par)
                    if not second and isinstance(k, int) and k == -1:
                        take_weights(1)
                        take_weights(2)
                span(act, -1 if second else -2, groups, 2, groups - 2, step)

            def rnn(k, par, on):
                if on(k):
                    act.wait_ge(gate_ready, k * 3 + 1)
                    if not isinstance(k, int) or k >= 2:
                        act.wait_ge(scan_done, k * 2 - 2)
                    nc.scalar.activation(relu_z[:, par, :], Z[par][0], ACT.Relu).then_inc(sig_done, 1)
                    for n in range(3):
                        if n:
                            act.wait_ge(gate_ready, k * 3 + n + 1)
                        nc.scalar.activation(sig[:, par, n, :], Z[par][n], ACT.Sigmoid).then_inc(sig_done, 1)
                if on(k + 1):
                    act.wait_ge(xt_ready, k + 1 + groups + 1)
                    if not isinstance(k, int) or k + 1 >= 2:
                        act.wait_ge(gate_ready, k * 3)
                    nc.scalar.copy(xt[:, 1 - par, :], T[:]).then_inc(xt_taken, 1)
                if on(k + 2) and not (isinstance(k, int) and k < 0):
                    norm(1, k + 2, par)

            ffn(False)
            act.preload_act_table(ACT.Sigmoid)
            span(act, -1, groups, 2, groups - 2, rnn)
            act.preload_act_table(ACT.Gelu)
            ffn(True)

        @block.tensor
        def _(pe):
            pe.wait_ge(consts_set, 6)
            pe.wait_ge(wsum_done, 2)
            pe.matmul(S[:, 0:2], ones[:], abs_sum[:], start=True, stop=True).then_inc(wtotal_done, 1)
            pe.wait_ge(ternary_done, 1)
            for c in range(chunks):
                t = pe.transpose(Y[:, 0, c, :], up_t[:, c * P:(c + 1) * P], ident[:])
            t.then_inc(w_turned, 1)

            def turn_more_weights():
                pe.wait_ge(ternary_done, 2)
                for c in range(chunks):
                    t = pe.transpose(Y[:, 1, c, :], down_t[:, c * P:(c + 1) * P], ident[:])
                t.then_inc(w_turned, 1)
                pe.wait_ge(w_gate_loaded, 48)
                for n in range(3):
                    t = pe.transpose(S[:, n * P:(n + 1) * P], gate_raw[:, n, :], ident[:])
                t.then_inc(w_turned, 1)

            def turn(g, par, base):
                pe.wait_ge(xn_ready, g + base + 1)
                if base or not isinstance(g, int) or g >= 1:
                    pe.wait_ge(xt_taken, g + base)
                for t in range(TILES):
                    m = pe.transpose(T[:, t * P:(t + 1) * P], xn[:, par, t, :], ident[:])
                m.then_inc(xt_ready, 1)

            def up(g, par, second):
                F = g + (groups if second else 0)
                pe.wait_ge(xt_taken, g + (2 * groups if second else 0) + 1)
                if not second and isinstance(g, int) and g == 0:
                    pe.wait_ge(w_taken, 1)
                for half in range(2):
                    if second or not isinstance(g, int) or g >= 1:
                        pe.wait_ge(gelu_done, F * 2 + half - 1)
                    for c in range(2):
                        f0 = (2 * half + c) * P
                        pe.matmul(U[half][:, c, :], up_w[:, f0:f0 + P], xt_hi[:, par, :], start=True, stop=False)
                        m = pe.matmul(U[half][:, c, :], up_w[:, f0:f0 + P], xt_lo[:, par, :], start=False, stop=True)
                    m.then_inc(up_ready, 1)

            def down(g, par, second):
                F = g + (groups if second else 0)
                pe.wait_ge(q_ready, F + 1)
                if not second and isinstance(g, int) and g == 0:
                    pe.wait_ge(w_taken, 3)
                if second or not isinstance(g, int) or g >= 1:
                    pe.wait_ge(ms_taken, F)
                for t in range(TILES):
                    m = pe.matmul(S[:, t:t + 1], q[:, par, t * P:(t + 1) * P], ones[:, 0:1], start=True, stop=True)
                m.then_inc(ssq_ready, 1)
                if second or not isinstance(g, int) or g >= 2:
                    pe.wait_ge(ffn_added, F - 1)
                for t in range(TILES):
                    for c in range(chunks):
                        m = pe.matmul(Y[:, par, t, :], h[:, par, c, t * P:(t + 1) * P], down_w[:, c, :],
                                      start=(c == 0), stop=(c == chunks - 1))
                m.then_inc(down_done, 1)

            def ffn(second):
                base = 2 * groups if second else 0

                def step(k, par, on):
                    if on(k) and not (second and isinstance(k, int) and k == 0):
                        up(k, par, second)
                    if on(k + 1) and not (second and isinstance(k, int) and k == 0):
                        turn(k + 1, 1 - par, base)
                    elif on(k) and not second:
                        turn(0, 0, groups)
                    if not second and isinstance(k, int) and k == -1:
                        turn_more_weights()
                    if on(k - 1):
                        if not second and isinstance(k, int) and k == groups:
                            gates(0, 0)
                            turn(1, 1, groups)
                        if second and isinstance(k, int) and k == 1:
                            pe.wait_ge(rnn_added, groups)
                        down(k - 1, 1 - par, second)

                span(pe, 0 if second else -1, groups + 1, 2, groups - 2, step)

            def gates(g, par):
                pe.wait_ge(xt_taken, g + groups + 1)
                if isinstance(g, int) and g == 0:
                    pe.wait_ge(gelu_done, 2 * groups)
                if not isinstance(g, int) or g >= 2:
                    pe.wait_ge(sig_done, g * 4 - 4)
                for n in range(3):
                    if isinstance(g, int) and g == 1 and n:
                        pe.wait_ge(ffn_added, groups - 2 + n)
                    pe.matmul(Z[par][n], gate_w[:, n, :], xt[:, par, :], start=True, stop=True).then_inc(gate_ready, 1)

            def rnn(k, par, on):
                if on(k) and not (isinstance(k, int) and k == 0):
                    gates(k, par)
                if isinstance(k, int) and k == groups + 1:
                    pe.wait_ge(sig_done, 4 * groups)
                    up(0, 0, True)
                    turn(1, 1, 2 * groups)
                if on(k - 2):
                    pe.wait_ge(scan_done, k * 2 - 2)
                    if isinstance(k, int) and k == 2:
                        pe.wait_ge(ms_taken, groups)
                    else:
                        pe.wait_ge(rnn_added, k - 2)
                    for t in range(TILES):
                        m = pe.transpose(O[:, t * P:(t + 1) * P], hidden[:, par, t * P:(t + 1) * P], ident[:])
                    m.then_inc(turned_back, 1)
                if on(k + 1) and not (isinstance(k, int) and k == 0):
                    turn(k + 1, 1 - par, groups)
                elif isinstance(k, int) and k == groups - 1:
                    turn(0, 0, 2 * groups)

            ffn(False)
            span(pe, 0, groups + 2, 4, groups - 2, rnn)
            ffn(True)

        @block.vector
        def _(dve):
            vec = nc.vector

            def weight_sum(n):
                dve.wait_ge((w_up_loaded, w_down_loaded)[n], 16)
                vec.tensor_reduce(abs_sum[:, n:n + 1], down_raw[:] if n else up_raw[:].rearrange("p c d -> p (c d)"),
                                  AXIS.X, ALU.add, apply_absolute_value=True).then_inc(wsum_done, 1)

            def weight_limits():
                dve.wait_ge(wtotal_done, 1)
                for n in range(2):
                    for sign in range(2):
                        m = vec.tensor_scalar(limit[:, 2 * n + sign:2 * n + sign + 1], S[:, n:n + 1],
                                              (0.5 if sign == 0 else -0.5) / (dff * d), None, ALU.mult)
                m.then_inc(limit_done, 1)
                dve.wait_ge(limit_done, 1)

            def ternary(n, raw, out):
                if n:
                    dve.wait_ge(ternary_done, n)
                vec.tensor_scalar(below[:], raw, limit[:, 2 * n + 1:2 * n + 2], None, ALU.is_lt).then_inc(below_done, 1)
                dve.wait_ge(below_done, n + 1)
                vec.scalar_tensor_tensor(out=out[:], in0=raw, scalar=limit[:, 2 * n:2 * n + 1], in1=below[:],
                                         op0=ALU.is_gt, op1=ALU.subtract).then_inc(ternary_done, 1)

            def bn(l, g, par, x_written, count):
                wait_alone(dve, (x_written, count))
                for t in range(TILES):
                    vec.bn_stats(st[l][:, par, t, :], X[:, tile_cols(g, 1, t), :])

            def mean_var(l, par):
                for t in range(TILES):
                    m = vec.bn_aggr(mv_now[l][:, par, t, :], st[l][:, par, t, :])
                m.then_inc(mv_done[l], 1)

            def ln_den_step(l, g, par):
                dve.wait_ge(root_done[l], g + 1)
                if l != 1:
                    vec.scalar_tensor_tensor(out=ln_den[:, par, :], in0=var_root[l][:, par, 0:4], scalar=RMS_EPS,
                                             in1=var_root[l][:, par, 4:8], op0=ALU.mult, op1=ALU.add).then_inc(den_done, 1)

            def ln_rstd_step(l, g, par, den_count):
                if l != 1:
                    dve.wait_ge(den_done, den_count)
                vec.reciprocal(rstd[l][:, tile_cols(g)],
                               var_root[l][:, par, 0:4] if l == 1 else ln_den[:, par, :]).then_inc(rstd_done[l], 1)

            def ln_shift_step(l, g, par):
                dve.wait_ge(rstd_done[l], g + 1)
                vec.scalar_tensor_tensor(out=shift[l][:, tile_cols(g)], in0=mv_now[l][:, par, :, 0], scalar=-1.0,
                                         in1=rstd[l][:, tile_cols(g)], op0=ALU.mult, op1=ALU.mult).then_inc(shift_done[l], 1)

            def norm(l, g, par):
                dve.wait_ge(shift_done[l], g + 1)
                dve.wait_ge(xt_ready, g + l * groups - 1)
                for t in range(TILES):
                    m = vec.tensor_scalar(xn[:, par, t, :], X[:, tile_cols(g, 1, t), :].rearrange("p a d -> p (a d)"),
                                          rstd[l][:, tile_cols(g, 1, t)], shift[l][:, tile_cols(g, 1, t)],
                                          ALU.mult, ALU.add)
                m.then_inc(xn_ready, 1)

            def low_part(g, par, l):
                dve.wait_ge(hi_ready, g + (groups if l else 0) + 1)
                vec.tensor_tensor(xt_lo[:, par, :], T[:], xt_hi[:, par, :], ALU.subtract).then_inc(xt_taken, 1)

            def sum_squares(F, half):
                dve.wait_ge(sq_done, F * 2 + half + 1)
                if not isinstance(F, int) or F >= 1:
                    dve.wait_ge(q_ready, F)
                vec.tensor_tensor(h_sq2[:, half, :], h_sq[:, 2 * half, :], h_sq[:, 2 * half + 1, :],
                                  ALU.add).then_inc(sq2_done, 1)

            def mean_square(F, par):
                dve.wait_ge(ssq_ready, F + 1)
                vec.tensor_scalar(ms[:, par, :], S[:, 0:TILES], 1.0 / dff, None, ALU.mult).then_inc(ms_taken, 1)

            def y_den_step(F, par):
                dve.wait_ge(rms_ready, F + 1)
                vec.tensor_scalar(rms_den[:, par, :], rms[:, par, :], RMS_EPS, 2.0, ALU.add, ALU.mult).then_inc(rms_den_done, 1)

            def y_scale_step(F, par):
                dve.wait_ge(rms_den_done, F + 1)
                vec.reciprocal(y_scale[:, par, :], rms_den[:, par, :]).then_inc(y_scale_done, 1)

            def y_add_step(F, g, par):
                dve.wait_ge(y_scale_done, F + 1)
                dve.wait_ge(down_done, F + 1)
                for t in range(TILES):
                    xt_ = X[:, tile_cols(g, 1, t), :].rearrange("p a d -> p (a d)")
                    m = vec.scalar_tensor_tensor(out=xt_, in0=Y[:, par, t, :], scalar=y_scale[:, par, t:t + 1], in1=xt_,
                                                 op0=ALU.mult, op1=ALU.add)
                m.then_inc(ffn_added, 1)

            def candidate(g, par):
                dve.wait_ge(sig_done, g * 4 + 2)
                if not isinstance(g, int) or g >= 2:
                    dve.wait_ge(inject_done, g - 1)
                vec.scalar_tensor_tensor(out=cand[:, par, :], in0=sig[:, par, 0, :], scalar=0.5, in1=relu_z[:, par, :],
                                         op0=ALU.min, op1=ALU.add).then_inc(cand_done, 1)

            def ffn1(k, par, on):
                if isinstance(k, int) and k == groups + 1:
                    candidate(0, 0)
                if on(k - 2):
                    y_den_step(k - 2, par)
                if on(k + 2):
                    ln_den_step(0, k + 2, par)
                if on(k - 2):
                    y_scale_step(k - 2, par)
                if on(k + 2):
                    ln_rstd_step(0, k + 2, par, k + 3)
                if on(k - 2):
                    y_add_step(k - 2, k - 2, par)
                if on(k + 2):
                    ln_shift_step(0, k + 2, par)
                if on(k - 2):
                    bn(1, k - 2, par, ffn_added, k - 1)
                if isinstance(k, int) and k == -4:
                    weight_sum(0)
                if isinstance(k, int) and k == -2:
                    ternary(1, down_raw[:], down_t)
                if on(k + 4):
                    bn(0, k + 4, par, x_loaded[par], (k + 4) * 8 + (8 if par else 16))
                if isinstance(k, int) and k == -4:
                    weight_sum(1)
                dve.drain()
                if on(k - 2):
                    mean_var(1, par)
                if on(k + 4):
                    mean_var(0, par)
                if on(k):
                    sum_squares(k, 0)
                if on(k - 3):
                    ln_den_step(1, k - 3, 1 - par)
                    ln_rstd_step(1, k - 3, 1 - par, 0)
                if on(k - 1):
                    mean_square(k - 1, 1 - par)
                if on(k + 1):
                    low_part(k + 1, 1 - par, 0)
                if on(k - 3):
                    ln_shift_step(1, k - 3, 1 - par)
                if on(k):
                    sum_squares(k, 1)
                if isinstance(k, int) and k == -4:
                    weight_limits()
                    ternary(0, up_raw[:].rearrange("p c d -> p (c d)"), up_t)

            def rnn(k, par, on):
                if isinstance(k, int) and groups - 1 <= k < groups + 1:
                    norm(2, k + 1 - groups, 1 - par)
                if on(k - 5):
                    ln_den_step(2, k - 5, 1 - par)
                if on(k - 3):
                    dve.wait_ge(turned_back, k - 2)
                    cols = tile_cols(k - 3)
                    vec.tensor_tensor(X[:, cols, :], O[:].rearrange("p (t d) -> p t d", d=d), X[:, cols, :],
                                      ALU.add).then_inc(rnn_added, 1)
                if on(k - 5):
                    ln_rstd_step(2, k - 5, 1 - par, groups + k - 4)
                if on(k - 3):
                    bn(2, k - 3, 1 - par, rnn_added, k - 2)
                if on(k - 5):
                    ln_shift_step(2, k - 5, 1 - par)
                if on(k - 3):
                    dve.drain()
                    mean_var(2, 1 - par)
                if on(k - 1):
                    dve.wait_ge(inject_done, k)
                    dve.wait_ge(sig_done, k * 4)
                    if not isinstance(k, int) or k >= 3:
                        dve.wait_ge(turned_back, k - 2)
                    for b in range(GT // seq):
                        cols = slice(b * seq, (b + 1) * seq)
                        vec.tensor_tensor_scan(hidden[:, 1 - par, cols], sig[:, 1 - par, 2, cols],
                                               inject[:, 1 - par, cols], 0.5, ALU.mult, ALU.add).then_inc(scan_done, 1)
                if on(k) and not (isinstance(k, int) and k == 0):
                    candidate(k, par)
                if isinstance(k, int) and k >= groups:
                    if k < groups + 2:
                        low_part(k - groups, par, 2)

            def ffn2(k, par, on):
                if on(k - 2):
                    y_den_step(k - 2 + groups, par)
                    y_scale_step(k - 2 + groups, par)
                if on(k):
                    sum_squares(k + groups, 0)
                if on(k - 2):
                    y_add_step(k - 2 + groups, k - 2, par)
                if on(k + 2):
                    norm(2, k + 2, par)
                if on(k - 1):
                    mean_square(k - 1 + groups, 1 - par)
                if on(k + 1) and not (isinstance(k, int) and k == 0):
                    low_part(k + 1, 1 - par, 2)
                if isinstance(k, int) and k < 2:
                    ln_den_step(2, k + groups - 2, par)
                    ln_rstd_step(2, k + groups - 2, par, 2 * groups - 1 + k)
                    ln_shift_step(2, k + groups - 2, par)
                if on(k):
                    sum_squares(k + groups, 1)

            span(dve, -4, groups + 3, 4, groups - 4, ffn1)
            span(dve, 1, groups + 3, 6, groups - 2, rnn)
            span(dve, 0, groups + 2, 2, groups - 2, ffn2)


def kernel(**inputs):
    import numpy as np
    import concourse.bacc as bacc
    from concourse.bass_utils import run_bass_kernel_spmd as run

    names = ["L0_attn_x", "L0_attn_Wf", "L0_attn_Wi", "L0_attn_Wh", "L0_ffn_w_up", "L0_ffn_w_down"]
    nc = bacc.Bacc("TRN2", target_bir_lowering=False, num_devices=1)
    arrays, args = {}, []
    for name in names:
        a = np.ascontiguousarray(inputs[name])
        arrays[f"in_{name}"] = a
        args.append(nc.dram_tensor(f"in_{name}", a.shape, mybir.dt.from_np(a.dtype), kind="ExternalInput").ap())
    out = nc.dram_tensor("out_x", arrays["in_L0_attn_x"].shape, F32, kind="ExternalOutput").ap()
    build_macaron(nc, *args, out)
    return run(nc, [arrays], core_ids=[0]).results[0]["out_x"]
```

```python
from contextlib import ExitStack

import concourse.bass as bass
from concourse import mybir

F32 = mybir.dt.float32
F16 = mybir.dt.float16
ALU = mybir.AluOpType
ACT = mybir.ActivationFunctionType
AXIS = mybir.AxisListType

P = 128
TILES = 4
GT = TILES * P
LN_EPS = 1e-5
RMS_EPS = 1e-8
H_SPLIT = 256.0
XN_SPLIT = 4096.0


def build_macaron(nc, x_in, w_f, w_i, w_h, w_up, w_down, x_out):
    batch, seq, d = x_in.shape
    dff = w_up.shape[0]
    chunks = dff // P
    groups = batch * seq // GT
    assert d == P and chunks == 4 and GT % seq == 0 and groups % 2 == 0
    x_src = x_in.rearrange("b s d -> (b s) d").rearrange("(n p) d -> p n d", p=P)
    x_dst = x_out.rearrange("b s d -> (b s) d").rearrange("(n p) d -> p n d", p=P)

    with ExitStack() as ctx:
        def sb(name, shape, dt=F32):
            return ctx.enter_context(nc.sbuf_tensor(name, shape, dt))

        def sem(name):
            return ctx.enter_context(nc.semaphore(name))

        X = sb("X", [P, groups * TILES, d])
        ident = sb("ident", [P, P])
        ones = sb("ones", [P, P])
        up_raw = sb("up_raw", [P, chunks, d])
        down_raw = sb("down_raw", [P, dff])
        gate_raw = sb("gate_raw", [P, 3, d])
        below = sb("below", [P, dff])
        up_t = sb("up_t", [P, dff])
        down_t = sb("down_t", [P, dff])
        abs_sum = sb("abs_sum", [P, 2])
        limit = sb("limit", [P, 4])
        up_w = sb("up_w", [P, dff], F16)
        down_w = sb("down_w", [P, chunks, d])
        gate_w = sb("gate_w", [P, 3, d])
        eps_tile = sb("eps_tile", [P, 3, TILES])
        root_exponent = sb("root_exponent", [P, 2 * TILES])
        st = [sb(f"st{l}", [P, 2, TILES, 6]) for l in range(3)]
        mv_now = [sb(f"mv_now{l}", [P, 2, TILES, 2]) for l in range(3)]
        rstd = [sb(f"rstd{l}", [P, groups * TILES]) for l in range(3)]
        shift = [sb(f"shift{l}", [P, groups * TILES]) for l in range(3)]
        var_eps = [sb(f"var_eps{l}", [P, 2, 8]) for l in range(3)]
        var_root = [sb(f"var_root{l}", [P, 2, 8]) for l in range(3)]
        ln_den = sb("ln_den", [P, 2, TILES])
        xn = sb("xn", [P, 2, TILES, d])
        xt_hi = sb("xt_hi", [P, 2, GT], F16)
        xt_lo = sb("xt_lo", [P, 2, GT], F16)
        h = sb("h", [P, 2, chunks, GT])
        h_hi = sb("h_hi", [P, 2, 2, GT], F16)
        h_lo = sb("h_lo", [P, 2, 2, GT], F16)
        down_w16 = sb("down_w16", [P, 2, d], F16)
        down_w256 = sb("down_w256", [P, 2, d])
        h_sq = sb("h_sq", [P, chunks, GT])
        h_sq2 = sb("h_sq2", [P, 2, GT])
        q = sb("q", [P, 2, GT])
        mean_sq = sb("mean_sq", [P, 2, TILES])
        rms = sb("rms", [P, 2, TILES])
        rms_den = sb("rms_den", [P, 2, TILES])
        y_scale = sb("y_scale", [P, 2, TILES])
        xt = sb("xt", [P, 2, GT])
        sig = sb("sig", [P, 2, 3, GT])
        cand = sb("cand", [P, 2, GT])
        inject = sb("inject", [P, 2, GT])
        hidden = sb("hidden", [P, 2, GT])

        T = ctx.enter_context(nc.psum_tensor("T", [P, GT], F32))
        S = ctx.enter_context(nc.psum_tensor("S", [P, GT], F32))
        U01 = ctx.enter_context(nc.psum_tensor("U01", [P, 2, GT], F32))
        U23 = ctx.enter_context(nc.psum_tensor("U23", [P, 2, GT], F32))
        Y = ctx.enter_context(nc.psum_tensor("Y", [P, 2, TILES, d], F32))
        U = [U01, U23]
        Z = [[U01[:, 0, :], U01[:, 1, :], U23[:, 0, :]],
             [U23[:, 1, :], Y[:, 0].rearrange("p t d -> p (t d)"), Y[:, 1].rearrange("p t d -> p (t d)")]]
        O = S

        x_loaded = [sem("x_loaded_even"), sem("x_loaded_odd")]
        x_stored = [sem("x_stored_even"), sem("x_stored_odd")]
        w_up_loaded, w_down_loaded, w_gate_loaded = sem("w_up_loaded"), sem("w_down_loaded"), sem("w_gate_loaded")
        consts_set, ident_zero = sem("consts_set"), sem("ident_zero")
        wsum_done, wtotal_done, limit_done = sem("wsum_done"), sem("wtotal_done"), sem("limit_done")
        below_done, ternary_done = sem("below_done"), sem("ternary_done")
        w_turned, up_w_taken, w_scaled = sem("w_turned"), sem("up_w_taken"), sem("w_scaled")
        other_w_taken = sem("other_w_taken")
        h_hi_done, h_lo_done = sem("h_hi_done"), sem("h_lo_done")
        mv_done = [sem(f"mv_done{l}") for l in range(3)]
        var_set = [sem(f"var_set{l}") for l in range(3)]
        root_done = [sem(f"root_done{l}") for l in range(3)]
        rstd_done = [sem(f"rstd_done{l}") for l in range(3)]
        shift_done = [sem(f"shift_done{l}") for l in range(3)]
        den_done, rms_den_done = sem("den_done"), sem("rms_den_done")
        xn_ready, xt_ready, xt_taken = sem("xn_ready"), sem("xt_ready"), sem("xt_taken")
        hi_ready, up_ready, gelu_done, sq_done = sem("hi_ready"), sem("up_ready"), sem("gelu_done"), sem("sq_done")
        sq2_done, q_ready = sem("sq2_done"), sem("q_ready")
        ssq_ready, mean_sq_done = sem("ssq_ready"), sem("mean_sq_done")
        rms_ready, y_scale_done = sem("rms_ready"), sem("y_scale_done")
        down_done, ffn_added = sem("down_done"), sem("ffn_added")
        gate_ready, sig_done, cand_done = sem("gate_ready"), sem("sig_done"), sem("cand_done")
        inject_done, scan_done = sem("inject_done"), sem("scan_done")
        turned_back, rnn_added = sem("turned_back"), sem("rnn_added")

        block = ctx.enter_context(nc.Block())

        def span(eng, start, stop, loop_from, loop_to, step):
            assert loop_from % 2 == 0 and loop_to % 2 == 0
            for k in range(start, loop_from):
                step(k, k % 2, lambda g: 0 <= g < groups)
            with eng.Fori(loop_from // 2, loop_to // 2) as pair:
                for j in range(2):
                    step(pair * 2 + j, j, lambda g: True)
            for k in range(loop_to, stop):
                step(k, k % 2, lambda g: 0 <= g < groups)

        def peeled(k, *steps):
            return isinstance(k, int) and k in steps

        def since(g, first):
            return not isinstance(g, int) or g >= first

        def wait_alone(eng, *waits):
            if not all(isinstance(value, int) for _, value in waits):
                waits = [(semaphore, eng.snap(value)) for semaphore, value in waits]
                eng.wait_ge(consts_set, 3)
            for semaphore, value in waits:
                eng.wait_ge(semaphore, value)

        def tile_cols(g, n=TILES, t=0):
            return bass.ds(g * TILES + t, n)

        @block.sync
        def _(sp):
            def load(g, par):
                sp.dma_start(X[:, tile_cols(g), :], x_src[:, tile_cols(g), :]).then_inc(x_loaded[par], 16)

            load(0, 0)
            load(1, 1)
            with sp.Fori(1, groups // 2) as pair:
                for j in range(2):
                    sp.wait_ge(x_loaded[j], pair * 16)
                    load(pair * 2 + j, j)
            with sp.Fori(0, groups // 2) as pair:
                for j in range(2):
                    sp.wait_ge(ffn_added, pair * 2 + (groups + 1 + j))
                    g = pair * 2 + j
                    sp.dma_start(x_dst[:, tile_cols(g), :], X[:, tile_cols(g), :]).then_inc(x_stored[j], 16)
            for j in range(2):
                sp.wait_ge(x_stored[j], 16 * (groups // 2))

        @block.gpsimd
        def _(pool):
            nc.gpsimd.memset(ident[:], 0.0).then_inc(ident_zero, 1)
            nc.gpsimd.memset(ones[:], 1.0).then_inc(consts_set, 1)
            nc.gpsimd.memset(root_exponent[:], 0.5).then_inc(consts_set, 1)
            for n, value in enumerate((LN_EPS, LN_EPS * XN_SPLIT ** -2, XN_SPLIT ** -2)):
                nc.gpsimd.memset(eps_tile[:, n, :], value).then_inc(consts_set, 1)
            pool.wait_ge(ident_zero, 1)
            nc.gpsimd.affine_select(out=ident[:], in_=ident[:], compare_op=ALU.not_equal, fill=1.0, base=0,
                                    pattern=[[-1, P]], channel_multiplier=1).then_inc(consts_set, 1)
            pool.wait_ge(consts_set, 6)

            def ln_roots(l, g, par):
                pool.wait_ge(mv_done[l], g + 1)
                var = mv_now[l][:, par, :, 1]
                if l == 1:
                    nc.gpsimd.tensor_tensor(var_eps[l][:, par, 0:4], var, eps_tile[:, 0, :], ALU.add).then_inc(var_set[l], 1)
                else:
                    nc.gpsimd.tensor_tensor(var_eps[l][:, par, 4:8], var, eps_tile[:, 2, :],
                                            ALU.mult).then_inc(var_set[l], 1)
                    pool.wait_ge(var_set[l], g * 2 + 1)
                    nc.gpsimd.tensor_tensor(var_eps[l][:, par, 0:4], var_eps[l][:, par, 4:8], eps_tile[:, 1, :],
                                            ALU.add).then_inc(var_set[l], 1)
                per = 1 if l == 1 else 2
                pool.wait_ge(var_set[l], g * per + per)
                nc.gpsimd.tensor_tensor(var_root[l][:, par, 0:4 * per], var_eps[l][:, par, 0:4 * per],
                                        root_exponent[:, 0:4 * per], ALU.pow).then_inc(root_done[l], 1)

            def rms_root(F, par):
                pool.wait_ge(mean_sq_done, F + 1)
                nc.gpsimd.tensor_tensor(rms[:, par, :], mean_sq[:, par, :], root_exponent[:, 0:TILES],
                                        ALU.pow).then_inc(rms_ready, 1)

            def add_squares(F, par):
                pool.wait_ge(sq2_done, F * 2 + 2)
                if since(F, 2):
                    pool.wait_ge(ssq_ready, F - 1)
                nc.gpsimd.tensor_tensor(q[:, par, :], h_sq2[:, 0, :], h_sq2[:, 1, :], ALU.add).then_inc(q_ready, 1)

            def ffn1(k, par, on):
                if on(k - 2):
                    ln_roots(1, k - 2, par)
                if on(k - 1):
                    rms_root(k - 1, 1 - par)
                if on(k):
                    add_squares(k, par)
                if on(k + 4):
                    ln_roots(0, k + 4, par)

            def rnn(k, par, on):
                if on(k):
                    pool.wait_ge(cand_done, k + 1)
                    pool.wait_ge(sig_done, k * 3 + 2)
                    nc.gpsimd.tensor_tensor(inject[:, par, :], sig[:, par, 1, :], cand[:, par, :],
                                            ALU.mult).then_inc(inject_done, 1)
                if on(k - 3):
                    ln_roots(2, k - 3, 1 - par)

            def ffn2(k, par, on):
                if on(k - 1):
                    rms_root(k - 1 + groups, 1 - par)
                if on(k):
                    add_squares(k + groups, par)

            span(pool, -4, groups + 2, 2, groups - 4, ffn1)
            span(pool, 0, groups + 3, 4, groups, rnn)
            span(pool, 0, groups + 1, 2, groups, ffn2)

        @block.scalar
        def _(act):
            nc.scalar.dma_start(up_raw[:], w_up.rearrange("(c p) d -> p c d", p=P)).then_inc(w_up_loaded, 16)
            nc.scalar.dma_start(down_raw[:], w_down).then_inc(w_down_loaded, 16)
            for n, w in enumerate((w_h, w_i, w_f)):
                nc.scalar.dma_start(gate_raw[:, n, :], w).then_inc(w_gate_loaded, 16)
            act.preload_act_table(ACT.Gelu)

            def norm(l, g, par):
                older = [(xt_ready, g + l * groups - 1)] if l or since(g, 2) else []
                wait_alone(act, (shift_done[l], g + 1), *older)
                for t in range(TILES):
                    m = nc.scalar.activation(xn[:, par, t, :], X[:, tile_cols(g, 1, t), :].rearrange("p a d -> p (a d)"),
                                             ACT.Identity, bias=shift[l][:, tile_cols(g, 1, t)],
                                             scale=rstd[l][:, tile_cols(g, 1, t)])
                m.then_inc(xn_ready, 1)

            def high_part(second, g, par):
                act.wait_ge(xt_ready, g + (2 * groups if second else 0) + 1)
                if second or since(g, 2):
                    act.wait_ge(up_ready, (g + (groups if second else 0)) * 2 - 2)
                nc.scalar.copy(xt_hi[:, par, :], T[:]).then_inc(hi_ready, 1)

            def ffn(second):
                off = groups if second else 0

                def gelu(g, par, half):
                    F = g + off
                    act.wait_ge(up_ready, F * 2 + half + 1)
                    if half == 0 and (second or since(g, 2)):
                        act.wait_ge(down_done, F - 1)
                    nc.scalar.activation(h[:, par, 2 * half:2 * half + 2, :], U[half][:], ACT.Gelu,
                                         scale=1.0 / XN_SPLIT).then_inc(gelu_done, 1)

                def square(g, par, half):
                    F = g + off
                    act.wait_ge(gelu_done, F * 2 + half + 1)
                    if second or since(g, 1):
                        act.wait_ge(sq2_done, F * 2 + half - 1)
                    nc.scalar.activation(h_sq[:, 2 * half:2 * half + 2, :], h[:, par, 2 * half:2 * half + 2, :],
                                         ACT.Square).then_inc(sq_done, 1)

                def split_high(g, par):
                    act.wait_ge(gelu_done, (g + off) * 2 + 1)
                    nc.scalar.mul(h_hi[:, par], h[:, par, 0:2, :], H_SPLIT).then_inc(h_hi_done, 1)

                def step(k, par, on):
                    if not second and peeled(k, -1):
                        norm(0, 0, 0)
                        act.wait_ge(w_turned, 1)
                        nc.scalar.copy(up_w[:], Y[:, 0].rearrange("p t d -> p (t d)")).then_inc(up_w_taken, 1)
                    early_square = not second and not peeled(k, 0)
                    if on(k):
                        gelu(k, par, 0)
                        if early_square:
                            square(k, par, 0)
                        gelu(k, par, 1)
                    if peeled(k, -1):
                        if not second:
                            high_part(second, 0, 0)
                    elif on(k + 1) and not (second and peeled(k, 0)):
                        high_part(second, k + 1, 1 - par)
                    elif on(k) and not second and not peeled(k, 0):
                        copy_turned(0, 0)
                    if on(k):
                        if second:
                            split_high(k, par)
                        if not early_square:
                            square(k, par, 0)
                        square(k, par, 1)
                    if on(k + 2) and not second:
                        norm(0, k + 2, par)
                    elif on(k) and not second:
                        norm(1, k + 2 - groups, par)
                    if second and peeled(k, -1):
                        high_part(second, 1, 1)
                span(act, -1, groups, 2, groups - 2, step)

            def copy_turned(g, par):
                act.wait_ge(xt_ready, g + groups + 1)
                if since(g, 2):
                    act.wait_ge(gate_ready, g * 3 - 3)
                nc.scalar.copy(xt[:, par, :], T[:]).then_inc(xt_taken, 1)

            def rnn(k, par, on):
                if on(k):
                    act.wait_ge(gate_ready, k * 3 + 1)
                    if since(k, 2):
                        act.wait_ge(scan_done, k * 2 - 2)
                    nc.scalar.activation(sig[:, par, 0, :], Z[par][0], ACT.Sigmoid).then_inc(sig_done, 1)
                if on(k + 1) and not peeled(k, -1):
                    copy_turned(k + 1, 1 - par)
                elif peeled(k, groups - 1):
                    high_part(True, 0, 0)
                if on(k):
                    for n in (1, 2):
                        act.wait_ge(gate_ready, k * 3 + n + 1)
                        nc.scalar.activation(sig[:, par, n, :], Z[par][n], ACT.Sigmoid).then_inc(sig_done, 1)
                if on(k + 3):
                    norm(1, k + 3, 1 - par)
                else:
                    norm(2, k + 3 - groups, 1 - par)

            ffn(False)
            act.preload_act_table(ACT.Sigmoid)
            span(act, -1, groups, 2, groups - 4, rnn)
            act.preload_act_table(ACT.Gelu)
            act.wait_ge(other_w_taken, 2)
            nc.scalar.copy(down_w16[:], down_w[:, 0:2, :]).then_inc(w_scaled, 1)
            nc.scalar.mul(down_w256[:], down_w[:, 2:4, :], H_SPLIT).then_inc(w_scaled, 1)
            ffn(True)

        @block.tensor
        def _(pe):
            pe.wait_ge(consts_set, 6)
            pe.wait_ge(wsum_done, 2)
            pe.matmul(S[:, 0:2], ones[:], abs_sum[:], start=True, stop=True).then_inc(wtotal_done, 1)
            pe.wait_ge(ternary_done, 1)
            for c in range(chunks):
                t = pe.transpose(Y[:, 0, c, :], up_t[:, c * P:(c + 1) * P], ident[:])
            t.then_inc(w_turned, 1)

            def turn_gate_weights():
                pe.wait_ge(w_gate_loaded, 48)
                pe.wait_ge(limit_done, 1)
                for n in range(3):
                    t = pe.transpose(S[:, n * P:(n + 1) * P], gate_raw[:, n, :], ident[:])
                t.then_inc(w_turned, 1)

            def turn_down_weights():
                pe.wait_ge(ternary_done, 2)
                for c in range(chunks):
                    t = pe.transpose(Y[:, 1, c, :], down_t[:, c * P:(c + 1) * P], ident[:])
                t.then_inc(w_turned, 1)

            def turn(g, par, base):
                pe.wait_ge(xn_ready, g + base + 1)
                if base or since(g, 1):
                    pe.wait_ge(xt_taken, g + base)
                for t in range(TILES):
                    m = pe.transpose(T[:, t * P:(t + 1) * P], xn[:, par, t, :], ident[:])
                m.then_inc(xt_ready, 1)

            def up(g, par, second):
                F = g + (groups if second else 0)
                pe.wait_ge(xt_taken, g + (2 * groups if second else 0) + 1)
                if not second and peeled(g, 0):
                    pe.wait_ge(up_w_taken, 1)
                for half in range(2):
                    if second or since(g, 1):
                        pe.wait_ge(gelu_done, F * 2 + half - 1)
                    if second and peeled(g, 0):
                        pe.wait_ge(sig_done, 3 * groups - 4 + 2 * half)
                        pe.wait_ge(cand_done, groups - 1 + half)
                    for c in range(2):
                        f0 = (2 * half + c) * P
                        pe.matmul(U[half][:, c, :], up_w[:, f0:f0 + P], xt_hi[:, par, :], start=True, stop=False)
                        m = pe.matmul(U[half][:, c, :], up_w[:, f0:f0 + P], xt_lo[:, par, :], start=False, stop=True)
                    m.then_inc(up_ready, 1)

            def sum_features(g, par, second):
                if not second and peeled(g, 0):
                    pe.wait_ge(other_w_taken, 2)
                F = g + (groups if second else 0)
                pe.wait_ge(q_ready, F + 1)
                if second or since(g, 1):
                    pe.wait_ge(mean_sq_done, F)
                for t in range(TILES):
                    m = pe.matmul(S[:, t:t + 1], q[:, par, t * P:(t + 1) * P], ones[:, 0:1], start=True, stop=True)
                m.then_inc(ssq_ready, 1)

            def down(g, par, second):
                F = g + (groups if second else 0)
                if second or since(g, 2):
                    pe.wait_ge(ffn_added, F - 1)
                if second:
                    pe.wait_ge(h_lo_done, g + 1)
                for t in range(TILES):
                    cols = slice(t * P, (t + 1) * P)
                    if second:
                        products = [(part[:, par, c, cols], down_w16[:, c, :]) for c in range(2) for part in (h_hi, h_lo)]
                        products += [(h[:, par, c, cols], down_w256[:, c - 2, :]) for c in range(2, chunks)]
                    else:
                        products = [(h[:, par, c, cols], down_w[:, c, :]) for c in range(chunks)]
                    for n, (tokens, weights) in enumerate(products):
                        m = pe.matmul(Y[:, par, t, :], tokens, weights, start=(n == 0), stop=(n == len(products) - 1))
                m.then_inc(down_done, 1)

            def ffn(second):
                base = 2 * groups if second else 0

                def step(k, par, on):
                    if on(k) and not (second and peeled(k, 0)):
                        up(k, par, second)
                    if on(k + 1) and not (second and peeled(k, 0)):
                        turn(k + 1, 1 - par, base)
                    elif on(k) and not second:
                        turn(0, 0, groups)
                    if not second and peeled(k, -1):
                        turn_gate_weights()
                    if not second and peeled(k, 0):
                        turn_down_weights()
                    if on(k - 1):
                        if not second and peeled(k, groups):
                            gates(0, 0)
                            turn(1, 1, groups)
                        if second and peeled(k, 1):
                            pe.wait_ge(rnn_added, groups)
                            pe.wait_ge(w_scaled, 2)
                        if not second:
                            sum_features(k - 1, 1 - par, second)
                        down(k - 1, 1 - par, second)
                        if second:
                            sum_features(k - 1, 1 - par, second)

                span(pe, 0 if second else -1, groups + 1, 2, groups - 2, step)

            def gates(g, par):
                pe.wait_ge(xt_taken, g + groups + 1)
                if peeled(g, 0):
                    pe.wait_ge(gelu_done, 2 * groups)
                if since(g, 2):
                    pe.wait_ge(sig_done, g * 3 - 3)
                    pe.wait_ge(cand_done, g - 1)
                for n in range(3):
                    if peeled(g, 1) and n:
                        pe.wait_ge(ffn_added, groups - 2 + n)
                    pe.matmul(Z[par][n], gate_w[:, n, :], xt[:, par, :], start=True, stop=True).then_inc(gate_ready, 1)

            def rnn(k, par, on):
                if on(k + 1) and not peeled(k, 0):
                    turn(k + 1, 1 - par, groups)
                elif peeled(k, groups - 1):
                    turn(0, 0, 2 * groups)
                if on(k) and not peeled(k, 0):
                    gates(k, par)
                if peeled(k, groups):
                    up(0, 0, True)
                    turn(1, 1, 2 * groups)
                if on(k - 2):
                    pe.wait_ge(scan_done, k * 2 - 2)
                    if peeled(k, 2):
                        pe.wait_ge(mean_sq_done, groups)
                    else:
                        pe.wait_ge(rnn_added, k - 2)
                    for t in range(TILES):
                        m = pe.transpose(O[:, t * P:(t + 1) * P], hidden[:, par, t * P:(t + 1) * P], ident[:])
                    m.then_inc(turned_back, 1)

            ffn(False)
            span(pe, 0, groups + 2, 4, groups - 2, rnn)
            ffn(True)

        @block.vector
        def _(dve):
            vec = nc.vector

            def weight_sum(n):
                dve.wait_ge((w_up_loaded, w_down_loaded)[n], 16)
                vec.tensor_reduce(abs_sum[:, n:n + 1], down_raw[:] if n else up_raw[:].rearrange("p c d -> p (c d)"),
                                  AXIS.X, ALU.add, apply_absolute_value=True).then_inc(wsum_done, 1)

            def weight_limits():
                dve.wait_ge(wtotal_done, 1)
                for n in range(2):
                    for sign in range(2):
                        m = vec.tensor_scalar(limit[:, 2 * n + sign:2 * n + sign + 1], S[:, n:n + 1],
                                              (0.5 if sign == 0 else -0.5) / (dff * d), None, ALU.mult)
                m.then_inc(limit_done, 1)
                dve.wait_ge(limit_done, 1)

            def ternary(n, raw, out):
                if n:
                    dve.wait_ge(ternary_done, n)
                vec.tensor_scalar(below[:], raw, limit[:, 2 * n + 1:2 * n + 2], None, ALU.is_lt).then_inc(below_done, 1)
                dve.wait_ge(below_done, n + 1)
                vec.scalar_tensor_tensor(out=out[:], in0=raw, scalar=limit[:, 2 * n:2 * n + 1], in1=below[:],
                                         op0=ALU.is_gt, op1=ALU.subtract).then_inc(ternary_done, 1)

            def take_gate_weights():
                dve.wait_ge(w_turned, 2)
                vec.tensor_copy(gate_w[:], S[:, 0:3 * d].rearrange("p (g d) -> p g d", d=d)).then_inc(other_w_taken, 1)

            def take_down_weights():
                dve.wait_ge(w_turned, 3)
                vec.tensor_copy(down_w[:], Y[:, 1]).then_inc(other_w_taken, 1)

            def bn(l, g, par, x_written, count):
                wait_alone(dve, (x_written, count))
                for t in range(TILES):
                    vec.bn_stats(st[l][:, par, t, :], X[:, tile_cols(g, 1, t), :])

            def mean_var(l, par):
                for t in range(TILES):
                    m = vec.bn_aggr(mv_now[l][:, par, t, :], st[l][:, par, t, :])
                m.then_inc(mv_done[l], 1)

            def ln_den_step(l, g, par):
                dve.wait_ge(root_done[l], g + 1)
                if l != 1:
                    vec.scalar_tensor_tensor(out=ln_den[:, par, :], in0=var_root[l][:, par, 0:4], scalar=RMS_EPS,
                                             in1=var_root[l][:, par, 4:8], op0=ALU.mult, op1=ALU.add).then_inc(den_done, 1)

            def ln_rstd_step(l, g, par, den_count):
                if l != 1:
                    dve.wait_ge(den_done, den_count)
                vec.reciprocal(rstd[l][:, tile_cols(g)],
                               var_root[l][:, par, 0:4] if l == 1 else ln_den[:, par, :]).then_inc(rstd_done[l], 1)

            def ln_shift_step(l, g, par):
                dve.wait_ge(rstd_done[l], g + 1)
                vec.scalar_tensor_tensor(out=shift[l][:, tile_cols(g)], in0=mv_now[l][:, par, :, 0], scalar=-1.0,
                                         in1=rstd[l][:, tile_cols(g)], op0=ALU.mult, op1=ALU.mult).then_inc(shift_done[l], 1)

            def norm(l, g, par):
                dve.wait_ge(shift_done[l], g + 1)
                dve.wait_ge(xt_ready, g + l * groups - 1)
                for t in range(TILES):
                    m = vec.tensor_scalar(xn[:, par, t, :], X[:, tile_cols(g, 1, t), :].rearrange("p a d -> p (a d)"),
                                          rstd[l][:, tile_cols(g, 1, t)], shift[l][:, tile_cols(g, 1, t)],
                                          ALU.mult, ALU.add)
                m.then_inc(xn_ready, 1)

            def low_part(g, par, l):
                dve.wait_ge(hi_ready, g + (groups if l else 0) + 1)
                vec.tensor_tensor(xt_lo[:, par, :], T[:], xt_hi[:, par, :], ALU.subtract).then_inc(xt_taken, 1)

            def split_low(g, par):
                dve.wait_ge(h_hi_done, g + 1)
                vec.scalar_tensor_tensor(out=h_lo[:, par], in0=h[:, par, 0:2, :], scalar=H_SPLIT, in1=h_hi[:, par],
                                         op0=ALU.mult, op1=ALU.subtract).then_inc(h_lo_done, 1)

            def sum_squares(F, half):
                dve.wait_ge(sq_done, F * 2 + half + 1)
                if since(F, 1):
                    dve.wait_ge(q_ready, F)
                vec.tensor_tensor(h_sq2[:, half, :], h_sq[:, 2 * half, :], h_sq[:, 2 * half + 1, :],
                                  ALU.add).then_inc(sq2_done, 1)

            def mean_square(F, par):
                dve.wait_ge(ssq_ready, F + 1)
                vec.tensor_scalar(mean_sq[:, par, :], S[:, 0:TILES], 1.0 / dff, None, ALU.mult).then_inc(mean_sq_done, 1)

            def y_den_step(F, par, times=2.0):
                dve.wait_ge(rms_ready, F + 1)
                vec.tensor_scalar(rms_den[:, par, :], rms[:, par, :], RMS_EPS, times,
                                  ALU.add, ALU.mult).then_inc(rms_den_done, 1)

            def y_scale_step(F, par):
                dve.wait_ge(rms_den_done, F + 1)
                vec.reciprocal(y_scale[:, par, :], rms_den[:, par, :]).then_inc(y_scale_done, 1)

            def y_add_step(F, g, par):
                dve.wait_ge(y_scale_done, F + 1)
                dve.wait_ge(down_done, F + 1)
                for t in range(TILES):
                    xt_ = X[:, tile_cols(g, 1, t), :].rearrange("p a d -> p (a d)")
                    m = vec.scalar_tensor_tensor(out=xt_, in0=Y[:, par, t, :], scalar=y_scale[:, par, t:t + 1], in1=xt_,
                                                 op0=ALU.mult, op1=ALU.add)
                m.then_inc(ffn_added, 1)

            def candidate(g, par):
                dve.wait_ge(sig_done, g * 3 + 1)
                if since(g, 2):
                    dve.wait_ge(inject_done, g - 1)
                vec.scalar_tensor_tensor(out=cand[:, par, :], in0=Z[par][0], scalar=0.5, in1=sig[:, par, 0, :],
                                         op0=ALU.add, op1=ALU.max).then_inc(cand_done, 1)

            def ffn1(k, par, on):
                if peeled(k, groups + 1):
                    candidate(0, 0)
                if on(k - 2):
                    y_den_step(k - 2, par)
                if on(k + 2):
                    ln_den_step(0, k + 2, par)
                if on(k - 2):
                    y_scale_step(k - 2, par)
                if on(k + 2):
                    ln_rstd_step(0, k + 2, par, k + 3)
                if on(k - 2):
                    y_add_step(k - 2, k - 2, par)
                if on(k + 2):
                    ln_shift_step(0, k + 2, par)
                if on(k - 2):
                    bn(1, k - 2, par, ffn_added, k - 1)
                if on(k + 4):
                    bn(0, k + 4, par, x_loaded[par], (k + 4) * 8 + (8 if par else 16))
                dve.drain()
                if on(k - 2):
                    mean_var(1, par)
                if on(k + 4):
                    mean_var(0, par)
                if peeled(k, 0):
                    take_gate_weights()
                    low_part(1, 1, 0)
                if on(k):
                    sum_squares(k, 0)
                if peeled(k, 0):
                    take_down_weights()
                if on(k - 3):
                    ln_den_step(1, k - 3, 1 - par)
                    ln_rstd_step(1, k - 3, 1 - par, 0)
                if on(k - 1):
                    mean_square(k - 1, 1 - par)
                if on(k + 1) and not peeled(k, 0):
                    low_part(k + 1, 1 - par, 0)
                if on(k - 3):
                    ln_shift_step(1, k - 3, 1 - par)
                if on(k):
                    sum_squares(k, 1)

            def rnn(k, par, on):
                if peeled(k, groups - 1):
                    low_part(0, 0, 2)
                    candidate(k, par)
                if on(k - 5):
                    ln_den_step(2, k - 5, 1 - par)
                if on(k - 3):
                    dve.wait_ge(turned_back, k - 2)
                    cols = tile_cols(k - 3)
                    vec.tensor_tensor(X[:, cols, :], O[:].rearrange("p (t d) -> p t d", d=d), X[:, cols, :],
                                      ALU.add).then_inc(rnn_added, 1)
                if on(k - 5):
                    ln_rstd_step(2, k - 5, 1 - par, groups + k - 4)
                if on(k - 3):
                    bn(2, k - 3, 1 - par, rnn_added, k - 2)
                if on(k - 5):
                    ln_shift_step(2, k - 5, 1 - par)
                if on(k - 3):
                    dve.drain()
                    mean_var(2, 1 - par)
                if peeled(k, groups):
                    low_part(1, 1, 2)
                if on(k - 1):
                    dve.wait_ge(inject_done, k)
                    dve.wait_ge(sig_done, k * 3)
                    if since(k, 3):
                        dve.wait_ge(turned_back, k - 2)
                    for b in range(GT // seq):
                        cols = slice(b * seq, (b + 1) * seq)
                        vec.tensor_tensor_scan(hidden[:, 1 - par, cols], sig[:, 1 - par, 2, cols],
                                               inject[:, 1 - par, cols], 0.5, ALU.mult, ALU.add).then_inc(scan_done, 1)
                if on(k) and not peeled(k, groups - 1):
                    candidate(k, par)

            def ffn2(k, par, on):
                if on(k + 2) and not peeled(k, 0):
                    norm(2, k + 2, par)
                if on(k - 2):
                    y_den_step(k - 2 + groups, par, 2.0 * H_SPLIT)
                    y_scale_step(k - 2 + groups, par)
                    y_add_step(k - 2 + groups, k - 2, par)
                if on(k + 1) and not peeled(k, 0):
                    low_part(k + 1, 1 - par, 2)
                if on(k):
                    split_low(k, par)
                if on(k - 1):
                    mean_square(k - 1 + groups, 1 - par)
                if peeled(k, 0, 1):
                    ln_den_step(2, k + groups - 2, par)
                    ln_rstd_step(2, k + groups - 2, par, 2 * groups - 1 + k)
                    ln_shift_step(2, k + groups - 2, par)
                if on(k):
                    sum_squares(k + groups, 0)
                    sum_squares(k + groups, 1)

            def ln_scales(g, par):
                ln_den_step(0, g, par)
                ln_rstd_step(0, g, par, g + 1)
                ln_shift_step(0, g, par)

            bn(0, 0, 0, x_loaded[0], 16)
            dve.drain()
            mean_var(0, 0)
            weight_sum(0)
            weight_sum(1)
            bn(0, 1, 1, x_loaded[1], 16)
            weight_limits()
            ln_scales(0, 0)
            ternary(0, up_raw[:].rearrange("p c d -> p (c d)"), up_t)
            dve.drain()
            mean_var(0, 1)
            bn(0, 2, 0, x_loaded[0], 32)
            low_part(0, 0, 0)
            ln_scales(1, 1)
            dve.drain()
            mean_var(0, 0)
            bn(0, 3, 1, x_loaded[1], 32)
            dve.drain()
            mean_var(0, 1)
            ternary(1, down_raw[:], down_t)
            span(dve, 0, groups + 3, 4, groups - 4, ffn1)
            span(dve, 1, groups + 3, 6, groups - 2, rnn)
            span(dve, 0, groups + 2, 2, groups - 2, ffn2)


def kernel(**inputs):
    import numpy as np
    import concourse.bacc as bacc
    from concourse.bass_utils import run_bass_kernel_spmd as run

    names = ["L0_attn_x", "L0_attn_Wf", "L0_attn_Wi", "L0_attn_Wh", "L0_ffn_w_up", "L0_ffn_w_down"]
    nc = bacc.Bacc("TRN2", target_bir_lowering=False, num_devices=1)
    arrays, args = {}, []
    for name in names:
        a = np.ascontiguousarray(inputs[name])
        arrays[f"in_{name}"] = a
        args.append(nc.dram_tensor(f"in_{name}", a.shape, mybir.dt.from_np(a.dtype), kind="ExternalInput").ap())
    out = nc.dram_tensor("out_x", arrays["in_L0_attn_x"].shape, F32, kind="ExternalOutput").ap()
    build_macaron(nc, *args, out)
    return run(nc, [arrays], core_ids=[0]).results[0]["out_x"]
```
